# Optimizing a Trainium2 kernel written in Bass

```python
import numpy as np
import jax
import jax.numpy as jnp

def _softmax(x, axis=-1):
    return jax.nn.softmax(x, axis=axis)

def _gelu(x):
    return jax.nn.gelu(x, approximate=True)

def _silu(x):
    return jax.nn.silu(x)

def _sigmoid(x):
    return jax.nn.sigmoid(x)

def _layernorm(x, axis=-1, eps=1e-05):
    m = jnp.mean(x, axis=axis, keepdims=True)
    v = jnp.var(x, axis=axis, keepdims=True)
    return (x - m) / jnp.sqrt(v + eps)

def _scatter_add(tgt, idx, src, axis=0):
    return tgt.at[idx].add(src)

def _segment_sum(src, seg, n):
    return jax.ops.segment_sum(src, seg, n)
kernel_name = 'mk_macaron_d1_jaxref_r8_6ba0c9'

def setup_inputs(seed: int=0):
    np.random.seed(seed)
    _w = jnp.asarray

    def _L0_attn_setup():
        import jax, jax.numpy as jnp
        import numpy as np
        N_HEADS = 16
        ROPE_BASE = 10000.0

        def _rope(x):
            B, L, H, Dh = x.shape
            half = Dh // 2
            inv_freq = 1.0 / ROPE_BASE ** (jnp.arange(0, half, dtype=jnp.float32) / half)
            ang = jnp.arange(L, dtype=jnp.float32)[:, None] * inv_freq[None, :]
            cos = jnp.concatenate([jnp.cos(ang), jnp.cos(ang)], axis=-1).astype(x.dtype)
            sin = jnp.concatenate([jnp.sin(ang), jnp.sin(ang)], axis=-1).astype(x.dtype)
            cos = cos[None, :, None, :]
            sin = sin[None, :, None, :]
            x1, x2 = (x[..., :half], x[..., half:])
            rot = jnp.concatenate([-x2, x1], axis=-1)
            return x * cos + rot * sin
        key = jax.random.key(seed)
        k1, k2, k3 = jax.random.split(key, 3)
        B, L, D = (2, 256, 128)
        x = jax.random.normal(k1, (B, L, D), dtype=jnp.float32)
        w_qkv = jax.random.normal(k2, (3 * D, D), dtype=jnp.float32) * D ** (-0.5)
        w_out = jax.random.normal(k3, (D, D), dtype=jnp.float32) * D ** (-0.5)
        return {'x': x, 'w_qkv': w_qkv, 'w_out': w_out}
    _L0_attn_in = _L0_attn_setup()

    def _L0_ffn_setup():
        import jax, jax.numpy as jnp
        import numpy as np
        B, S, DIM = (4, 512, 128)
        BASE_COUPLING = 0.1
        NUM_CYCLES = 3

        def _gelu(x):
            return jax.nn.gelu(x, approximate=False)

        def _coupling_net(h, w1, b1, w2, b2, w3, b3, w4, b4):
            h = _gelu(h @ w1 + b1)
            h = _gelu(h @ w2 + b2)
            h = _gelu(h @ w3 + b3)
            return jax.nn.sigmoid(h @ w4 + b4)

        def _global_net(h, w1, b1, w2, b2, w3, b3):
            h = _gelu(h @ w1 + b1)
            h = _gelu(h @ w2 + b2)
            return jax.nn.sigmoid(h @ w3 + b3)

        def _twist(x):
            o_r, o_i, p_r, p_i = jnp.split(x, 4, axis=-1)
            return jnp.concatenate([p_r, -p_i, -o_r, o_i], axis=-1)
        key = jax.random.key(seed)
        ks = jax.random.split(key, 9)
        d = DIM

        def w(k, fan_in, fan_out):
            return jax.random.normal(k, (fan_in, fan_out), dtype=jnp.float32) / np.sqrt(fan_in).astype(np.float32)
        inp = {'x': jax.random.normal(ks[0], (B, S, d), dtype=jnp.float32)}
        cn_dims = [(d, d), (d, d // 2), (d // 2, d // 4), (d // 4, 1)]
        for i, (a, b) in enumerate(cn_dims):
            inp[f'cn_w{i + 1}'] = w(ks[1 + i], a, b)
            inp[f'cn_b{i + 1}'] = jnp.zeros((b,), dtype=jnp.float32)
        gc_dims = [(d, d // 2), (d // 2, d // 4), (d // 4, 1)]
        for i, (a, b) in enumerate(gc_dims):
            inp[f'gc_w{i + 1}'] = w(ks[5 + i], a, b)
            inp[f'gc_b{i + 1}'] = jnp.zeros((b,), dtype=jnp.float32)
        inp['adaptive_range'] = jnp.full((1,), 0.2, dtype=jnp.float32)
        return inp
    _L0_ffn_in = _L0_ffn_setup()
    _d = {'L0_attn_x': _L0_attn_in['x'], 'L0_attn_w_qkv': _L0_attn_in['w_qkv'], 'L0_attn_w_out': _L0_attn_in['w_out'], 'L0_ffn_cn_w1': _L0_ffn_in['cn_w1'], 'L0_ffn_cn_b1': _L0_ffn_in['cn_b1'], 'L0_ffn_cn_w2': _L0_ffn_in['cn_w2'], 'L0_ffn_cn_b2': _L0_ffn_in['cn_b2'], 'L0_ffn_cn_w3': _L0_ffn_in['cn_w3'], 'L0_ffn_cn_b3': _L0_ffn_in['cn_b3'], 'L0_ffn_cn_w4': _L0_ffn_in['cn_w4'], 'L0_ffn_cn_b4': _L0_ffn_in['cn_b4'], 'L0_ffn_gc_w1': _L0_ffn_in['gc_w1'], 'L0_ffn_gc_b1': _L0_ffn_in['gc_b1'], 'L0_ffn_gc_w2': _L0_ffn_in['gc_w2'], 'L0_ffn_gc_b2': _L0_ffn_in['gc_b2'], 'L0_ffn_gc_w3': _L0_ffn_in['gc_w3'], 'L0_ffn_gc_b3': _L0_ffn_in['gc_b3'], 'L0_ffn_adaptive_range': _L0_ffn_in['adaptive_range']}
    _x0 = _d['L0_attn_x']
    _d['L0_attn_x'] = jax.random.normal(jax.random.fold_in(jax.random.key(seed), 1), (8, 512, 128), dtype=_x0.dtype)
    del _x0
    return _d

def reference(L0_attn_x, L0_attn_w_qkv, L0_attn_w_out, L0_ffn_cn_w1, L0_ffn_cn_b1, L0_ffn_cn_w2, L0_ffn_cn_b2, L0_ffn_cn_w3, L0_ffn_cn_b3, L0_ffn_cn_w4, L0_ffn_cn_b4, L0_ffn_gc_w1, L0_ffn_gc_b1, L0_ffn_gc_w2, L0_ffn_gc_b2, L0_ffn_gc_w3, L0_ffn_gc_b3, L0_ffn_adaptive_range):

    def _L0_attn_ref(x, w_qkv, w_out):
        import jax, jax.numpy as jnp
        import numpy as np
        N_HEADS = 16
        ROPE_BASE = 10000.0

        def _rope(x):
            B, L, H, Dh = x.shape
            half = Dh // 2
            inv_freq = 1.0 / ROPE_BASE ** (jnp.arange(0, half, dtype=jnp.float32) / half)
            ang = jnp.arange(L, dtype=jnp.float32)[:, None] * inv_freq[None, :]
            cos = jnp.concatenate([jnp.cos(ang), jnp.cos(ang)], axis=-1).astype(x.dtype)
            sin = jnp.concatenate([jnp.sin(ang), jnp.sin(ang)], axis=-1).astype(x.dtype)
            cos = cos[None, :, None, :]
            sin = sin[None, :, None, :]
            x1, x2 = (x[..., :half], x[..., half:])
            rot = jnp.concatenate([-x2, x1], axis=-1)
            return x * cos + rot * sin
        B, L, D = x.shape
        H = N_HEADS
        Dh = D // H
        qkv = jnp.einsum('bld,ed->ble', x, w_qkv)
        q, k, v = jnp.split(qkv, 3, axis=-1)
        q = q.reshape(B, L, H, Dh)
        k = k.reshape(B, L, H, Dh)
        v = v.reshape(B, L, H, Dh)
        q = _rope(q)
        k = _rope(k)
        scale = 1.0 / jnp.sqrt(jnp.asarray(Dh, dtype=x.dtype))
        scores = jnp.einsum('blhd,bmhd->bhlm', q, k) * scale
        attn = jax.nn.softmax(scores, axis=-1)
        out = jnp.einsum('bhlm,bmhd->blhd', attn, v).reshape(B, L, D)
        return jnp.einsum('bld,ed->ble', out, w_out)

    def _L0_ffn_ref(x, cn_w1, cn_b1, cn_w2, cn_b2, cn_w3, cn_b3, cn_w4, cn_b4, gc_w1, gc_b1, gc_w2, gc_b2, gc_w3, gc_b3, adaptive_range):
        import jax, jax.numpy as jnp
        import numpy as np
        B, S, DIM = (4, 512, 128)
        BASE_COUPLING = 0.1
        NUM_CYCLES = 3

        def _gelu(x):
            return jax.nn.gelu(x, approximate=False)

        def _coupling_net(h, w1, b1, w2, b2, w3, b3, w4, b4):
            h = _gelu(h @ w1 + b1)
            h = _gelu(h @ w2 + b2)
            h = _gelu(h @ w3 + b3)
            return jax.nn.sigmoid(h @ w4 + b4)

        def _global_net(h, w1, b1, w2, b2, w3, b3):
            h = _gelu(h @ w1 + b1)
            h = _gelu(h @ w2 + b2)
            return jax.nn.sigmoid(h @ w3 + b3)

        def _twist(x):
            o_r, o_i, p_r, p_i = jnp.split(x, 4, axis=-1)
            return jnp.concatenate([p_r, -p_i, -o_r, o_i], axis=-1)
        global_context = x.mean(axis=1, keepdims=True)
        gf = _global_net(global_context, gc_w1, gc_b1, gc_w2, gc_b2, gc_w3, gc_b3)
        out = x
        for _ in range(NUM_CYCLES):
            tf = _coupling_net(out, cn_w1, cn_b1, cn_w2, cn_b2, cn_w3, cn_b3, cn_w4, cn_b4)
            combined = 0.7 * gf + 0.3 * tf
            coupling = BASE_COUPLING + adaptive_range * (combined - 0.5) * 2.0
            out = out + coupling * _twist(out)
        return out
    x = L0_attn_x
    x = x + 0.5 * _L0_ffn_ref(_layernorm(x, axis=-1), L0_ffn_cn_w1, L0_ffn_cn_b1, L0_ffn_cn_w2, L0_ffn_cn_b2, L0_ffn_cn_w3, L0_ffn_cn_b3, L0_ffn_cn_w4, L0_ffn_cn_b4, L0_ffn_gc_w1, L0_ffn_gc_b1, L0_ffn_gc_w2, L0_ffn_gc_b2, L0_ffn_gc_w3, L0_ffn_gc_b3, L0_ffn_adaptive_range)
    x = x + _L0_attn_ref(_layernorm(x, axis=-1), L0_attn_w_qkv, L0_attn_w_out)
    x = x + 0.5 * _L0_ffn_ref(_layernorm(x, axis=-1), L0_ffn_cn_w1, L0_ffn_cn_b1, L0_ffn_cn_w2, L0_ffn_cn_b2, L0_ffn_cn_w3, L0_ffn_cn_b3, L0_ffn_cn_w4, L0_ffn_cn_b4, L0_ffn_gc_w1, L0_ffn_gc_b1, L0_ffn_gc_w2, L0_ffn_gc_b2, L0_ffn_gc_w3, L0_ffn_gc_b3, L0_ffn_adaptive_range)
    return x

_drawn_inputs = setup_inputs


def setup_inputs(seed=0):
    import zlib

    import numpy as np

    out = dict(_drawn_inputs(seed))
    spreads = {'L0_ffn_cn_b1': (0.0, 0.8),
     'L0_ffn_cn_b2': (0.0, 2.0),
     'L0_ffn_cn_b3': (0.0, 2.0),
     'L0_ffn_gc_b1': (0.0, 2.0),
     'L0_ffn_gc_b2': (0.0, 2.0)}
    factors = {'L0_ffn_cn_w1': 7.024,
     'L0_ffn_cn_w2': 6.621,
     'L0_ffn_cn_w3': 5.711,
     'L0_ffn_cn_w4': 3.652,
     'L0_ffn_gc_w1': 64.0,
     'L0_ffn_gc_w2': 64.0,
     'L0_ffn_gc_w3': 8.0}
    for name, (base, spread) in spreads.items():
        noise = np.random.default_rng([zlib.crc32(name.encode()), seed]).standard_normal(out[name].shape)
        drawn = base * np.exp(spread * noise) if base else spread * noise
        out[name] = jnp.asarray(drawn.astype(out[name].dtype))
    for name, factor in factors.items():
        out[name] = (out[name] * factor).astype(out[name].dtype)
    return out
```

```python
from contextlib import ExitStack

import concourse.bass as bass
from concourse import mybir

P = 128
F32 = mybir.dt.float32
BF16 = mybir.dt.bfloat16
ALU = mybir.AluOpType
ACT = mybir.ActivationFunctionType
AX_X = mybir.AxisListType.X

EPS = 1e-5
BASE_COUPLING = 0.1
GF_SHARE, TF_SHARE = 0.7, 0.3
CYCLES = 3

Q_PARTS = [0, 0, 0, 1, 1, 2]
K_PARTS = [0, 1, 2, 0, 1, 0]
TERMS = len(Q_PARTS)


def macaron_kernel(nc, x, w_qkv, w_out, cn, gc, adaptive_range, cos_t, sin_t, ident_t, out):
    B, S, D = x.shape
    H, DH = 16, D // 16
    T = S // P
    HP = H // 2
    HALF = H // 2
    PAIRS = HALF // 2
    G = B // 4
    MAX_ROW = TERMS * DH
    SCALE = float(DH) ** -0.5
    VC = 32
    (w1, b1, w2, b2, w3, b3, w4, b4), (g1, gb1, g2, gb2, g3, gb3) = cn, gc

    with ExitStack() as ctx:
        def sb(name, shape, dt=F32):
            return ctx.enter_context(nc.sbuf_tensor(name, shape, dt))

        def sem(name):
            return ctx.enter_context(nc.semaphore(name))

        ps = ctx.enter_context(nc.psum_tensor("ps", [P, 8, 512], F32))

        xs = sb("xs", [P, B, T, D])
        st = sb("st", [P, B, T, D])
        ident = sb("ident", [P, P])
        ident_bf = sb("ident_bf", [P, P], BF16)
        cosb, sinb = sb("cosb", [P, S]), sb("sinb", [P, S])
        w1s, w2s, w3s = sb("w1s", [P, 128]), sb("w2s", [P, 64]), sb("w3s", [P, 64])
        w4s = sb("w4s", [P, 4])
        g1s, g2s, g3s, g3r = sb("g1s", [P, 64]), sb("g2s", [64, 32]), sb("g3s", [32, 1]), sb("g3r", [32, P])
        b1s, b2s, b3s, b4s = sb("b1s", [P, 1]), sb("b2s", [P, 1]), sb("b3s", [P, 1]), sb("b4s", [P, 1])
        gb1s, gb2s, gb3s = sb("gb1s", [64, 1]), sb("gb2s", [32, 1]), sb("gb3s", [P, 1])
        b4h, gb3h = sb("b4h", [P, 1]), sb("gb3h", [P, 1])
        ar, ar_tf, ar_gf = sb("ar", [P, 1]), sb("ar_tf", [P, 1]), sb("ar_gf", [P, 1])
        ones = sb("ones", [P, 1])
        wT = sb("wT", [P, 4, D])
        stats, mv = sb("stats", [P, B, T, 6]), sb("mv", [P, B, T, 2])
        var, rstd, minus_half = sb("var", [P, B, T]), sb("rstd", [P, B, T]), sb("minus_half", [P, B, T])
        gm, gh1, gh2, gth = sb("gm", [P, B]), sb("gh1", [64, B]), sb("gh2", [32, B]), sb("gth", [P, B])
        s0 = sb("s0", [P, B])
        th = sb("th", [P, G, 4, T])
        cs = sb("cs", [P, G, 3, 4 * T])
        big = sb("big", [P, 8, T * S])
        xT = big[:, 0:2, :].rearrange("p g (b s) -> p g b s", b=4)
        h1 = big[:, 2:4, :].rearrange("p g (b s) -> p g b s", b=4)
        tmp = big[:, 4:6, :].rearrange("p g (b t d) -> p g b t d", b=4, t=T)
        h2 = big[:, 6, :].rearrange("p (g b s) -> p g b s", g=2, b=2)
        h3 = big[:, 7, 0:2 * S].rearrange("p (g s) -> p g s", g=2)
        wnat = big[:, 7, 2 * S:2 * S + 4 * D].rearrange("p (a d) -> p a d", a=4)
        probs = big
        oT = st[:, 0:4].rearrange("p g t d -> p g (t d)")
        oT0 = sb("oT0", [P, S])
        on = st[:, 4]
        onT = st[:, 5].rearrange("p t d -> p (t d)")
        xn = st[:, 6:8]
        xnT = sb("xnT", [P, 2, S])
        qf, kf, qsw, ksw = sb("qf", [P, S]), sb("kf", [P, S]), sb("qsw", [P, S]), sb("ksw", [P, S])
        ra, rb, rc, rd = sb("ra", [P, S]), sb("rb", [P, S]), sb("rc", [P, S]), sb("rd", [P, S])
        qp, kp = sb("qp", [P, 3, S], BF16), sb("kp", [P, 3, S], BF16)
        qst = sb("qst", [P, 2, HP, S], BF16)
        kst = sb("kst", [P, 2, H, S], BF16)
        zrow = sb("zrow", [3, PAIRS * S], BF16)
        orow = sb("orow", [3, S], BF16)
        vst = sb("vst", [P, 2, T, H, VC])
        nmax = sb("nmax", [P, 2, T, 2, PAIRS])
        nres = sb("nres", [P, T, 2, PAIRS])
        nparts = sb("nparts", [P, T, 2, 3, PAIRS], BF16)
        mrow = sb("mrow", [6 * PAIRS, S], BF16)
        rden = sb("rden", [P, T, H])

        S_ = {}
        for name in (
            "ident_in half_ready ln_var x_in0 x_in1 w_in cst_in wc_in st_out setup_dve setup_pool ones_dma ident_ready halves "
            "wT_ready wT_copied ln_stats ln_mv ln_rstd ln_out gm_ready gm_copied gh1_ready gh1_done gh2_ready "
            "gh2_done gth_ready gth_done s0_ready x_new "
            "xn_ready xT_ready xnT_done q_ready q_done k_ready k_done v_ready v_done qsw_in ksw_in rope_a rope_b "
            "rope_c part1 res1 part2 parts_ready fill0 fill1 st_ready st_used s_ready s_used "
            "exp_done pv_ready pv_used pv_step n1 nr1 n2 n3 maxT_ready maxT_done mrow_out0 mrow_out1 "
            "oT_ready oT_rden oT_used on_done onT_ready onT_done proj_ready proj_done kept0 kept1"
        ).split():
            S_[name] = sem(name)
        for g in range(G):
            for name in "T_ready T_copied L1_ready h1_done L2_ready h2_done L3_ready h3_done L4_ready th_done cs0 cs1 cs_ready mul_done upd_dve mul_pool upd_pool".split():
                S_[name, g] = sem(f"{name}_{g}")

        def s(name, g=None):
            return S_[name] if g is None else S_[name, g]

        x_dram = x.rearrange("b (t p) d -> p b t d", p=P)
        out_dram = out.rearrange("b (t p) d -> p b t d", p=P)
        col = lambda v: v.rearrange("(p a) -> p a", a=1)

        def waits_for(eng, semaphore, count):
            if not isinstance(count, int) or count > 0:
                eng.wait_ge(semaphore, count)

        block = ctx.enter_context(nc.Block())
        WC_DMAS = 24
        SWAP_ROWS = PAIRS * DH // 2
        SWAP = 16 * P // SWAP_ROWS
        FILL = 16 * 2 * (2 * TERMS + 1)

        def pipeline(eng, iteration):
            for i in (-2, -1, 0, 1):
                iteration(i, i % 2, i, i)
            with eng.Fori(1, B // 2 - 1) as j:
                for q in range(2):
                    iteration(2 * j + q, q, 2, B - 3)
            for i in (B - 2, B - 1, B):
                iteration(i, i % 2, i, i)

        def output_T(g, q):
            return oT0[:] if g == 0 and q else oT[:, g]

        def coupling(g, k, a):
            v = cs[:, g, a:a + 2, k]
            return v.rearrange("p u t -> p t u").unsqueeze(3).to_broadcast([P, k.stop - k.start, 2, 32])

        @block.sync
        def _(sp):
            for g in range(G):
                sp.dma_start(xs[:, 4 * g:4 * g + 4], x_dram[:, 4 * g:4 * g + 4]).then_inc(s(f"x_in{g}"), 16)
                if g == 0:
                    sp.dma_start(ident[:], ident_t).then_inc(s("ident_in"), 16)

            def small(dst, src):
                sp.dma_start(dst, src).then_inc(s("wc_in"), 16)

            sp.wait_ge(s("setup_dve"), 1)
            jobs = [(w1s[:], w1), (w2s[:], w2), (b1s[:], col(b1)), (g1s[:], g1), (g2s[:], g2), (g3s[:], g3),
                    (gb1s[:], col(gb1)), (gb2s[:], col(gb2)),
                    (b4s[:], b4.partition_broadcast(P)), (gb3s[:], gb3.partition_broadcast(P)),
                    (ar[:], adaptive_range.partition_broadcast(P))]
            jobs += [(b2s[64 * i:64 * i + 64], col(b2)) for i in range(2)]
            jobs += [(b3s[32 * i:32 * i + 32], col(b3)) for i in range(4)]
            jobs += [(w3s[64 * i:64 * i + 64, 32 * i:32 * i + 32], w3) for i in range(2)]
            jobs += [(w4s[32 * i:32 * i + 32, i:i + 1], w4) for i in range(4)]
            assert len(jobs) == WC_DMAS - 1
            for dst, src in jobs:
                small(dst, src)
            small(wnat[:, 3], w_out)
            for j in range(2):
                src = w_qkv[j * D:(j + 1) * D].rearrange("(f hp par d) c -> par f d hp c", f=2, par=2, d=DH)
                for par in range(2):
                    for f in range(2):
                        r = 64 * par + 32 * f
                        sp.dma_start(wnat[r:r + 32, j], src[par, f]).then_inc(s("w_in"), 16)
            sp.dma_start(wnat[:, 2], w_qkv[2 * D:3 * D]).then_inc(s("w_in"), 16)
            sp.dma_start(cosb[:], cos_t).then_inc(s("cst_in"), 16)
            sp.dma_start(sinb[:], sin_t).then_inc(s("cst_in"), 16)
            sp.wait_ge(s("setup_pool"), 1)
            for q in range(2):
                for par in range(2):
                    r = 64 * par + MAX_ROW
                    sp.dma_start(kst[r:r + 3, q].rearrange("p (hp two) c -> p hp two c", two=2)[:, :, par, :],
                                 orow[:].unsqueeze(1).to_broadcast([3, HP, S])).then_inc(s("ones_dma"), 16)

            def swap(b, k, f, sw):
                sp.wait_ge(s("qk"[k] + "_done"), b + 1)
                for r in range(0, P, 2 * SWAP_ROWS):
                    for lo, hi in ((r, r + SWAP_ROWS), (r + SWAP_ROWS, r)):
                        sp.dma_start(sw[lo:lo + SWAP_ROWS], f[hi:hi + SWAP_ROWS]).then_inc(s("qk"[k] + "sw_in"), 16)

            def fill(b, q, half):
                if half == 0:
                    sp.wait_ge(s("parts_ready"), 2 * b + 2)
                elif not isinstance(b, int) or b >= 2:
                    sp.wait_ge(s("st_ready"), 2 * H * (b - 1))
                for par in range(2):
                    h0 = slice(PAIRS * half, PAIRS * (half + 1))
                    for t in range(TERMS):
                        r = 64 * par + t * DH
                        p0 = 64 * par + PAIRS * DH * half
                        kdst = kst[r:r + DH, q].rearrange("p (hp two) c -> p hp two c", two=2)[:, h0, par, :]
                        sp.dma_start(qst[r:r + DH, q, h0, :], qp[p0:p0 + PAIRS * DH, Q_PARTS[t], :])\
                            .then_inc(s(f"fill{half}"), 16)
                        sp.dma_start(kdst, kp[p0:p0 + PAIRS * DH, K_PARTS[t], :]).then_inc(s(f"fill{half}"), 16)
                    r = 64 * par + MAX_ROW
                    sp.dma_start(qst[r:r + 3, q, h0, :].rearrange("p h c -> p (h c)"), zrow[:])\
                        .then_inc(s(f"fill{half}"), 16)

            def max_rows(b, q, half):
                sp.wait_ge(s("maxT_done"), 2 * b + half + 1)
                for par in range(2):
                    r = 64 * par + MAX_ROW
                    sp.dma_start(qst[r:r + 3, q, PAIRS * half:PAIRS * (half + 1), :],
                                 mrow[3 * PAIRS * par:3 * PAIRS * (par + 1), :]).then_inc(s(f"mrow_out{half}"), 16)

            def iteration(i, q, first, last):
                if first >= -1 and last <= B - 2:
                    fill(i + 1, 1 - q, 1)
                if last <= B - 3:
                    swap(i + 2, 0, qf, qsw)
                if first >= 0 and last <= B - 1:
                    max_rows(i, q, 1)
                if last <= B - 3:
                    swap(i + 2, 1, kf, ksw)
                if first >= -1 and last <= B - 2:
                    max_rows(i + 1, 1 - q, 0)
                if last <= B - 3:
                    fill(i + 2, q, 0)

            pipeline(sp, iteration)

            for b in range(B):
                sp.wait_ge(s("x_new"), B + b + 1)
                sp.dma_start(out_dram[:, b], xs[:, b]).then_inc(s("st_out"), 16)
            sp.wait_ge(s("st_out"), 16 * B)

        @block.gpsimd
        def _(pool):
            nc.gpsimd.memset(minus_half[:], -0.5).then_inc(s("half_ready"), 1)
            nc.gpsimd.memset(orow[:], 1.0)
            nc.gpsimd.memset(zrow[:], 0.0)
            nc.gpsimd.memset(qst[:].rearrange("p q h c -> p (q h c)").bitcast(F32), 0.0)
            nc.gpsimd.memset(kst[:].rearrange("p q h c -> p (q h c)").bitcast(F32), 0.0).then_inc(s("setup_pool"), 1)

            def update(it, g):
                pool.wait_ge(s("cs_ready", g), it + 1)
                b, k = 4 * g + 3, slice(3 * T, 4 * T)
                for a in range(2):
                    last = nc.gpsimd.tensor_tensor(
                        tmp[:, g, 3, :, 64 * a:64 * a + 64].rearrange("p t (u d) -> p t u d", u=2),
                        st[:, b, :, 64 - 64 * a:128 - 64 * a].rearrange("p t (u d) -> p t u d", u=2),
                        coupling(g, k, a), ALU.mult)
                last.then_inc(s("mul_pool", g), 1)
                pool.wait_ge(s("mul_pool", g), it + 1)
                nc.gpsimd.tensor_tensor(st[:, b], st[:, b], tmp[:, g, 3], ALU.add).then_inc(s("upd_pool", g), 1)

            def invert(call, slots):
                pool.wait_ge(s("ln_var"), call + 1)
                nc.gpsimd.tensor_tensor(rstd[:, slots], var[:, slots], minus_half[:, slots], ALU.pow)\
                    .then_inc(s("ln_rstd"), 1)

            def feed_forward(n):
                for g in range(G):
                    invert((G + B) * n + g, slice(4 * g, 4 * g + 4))
                with pool.Fori(0, CYCLES) as c:
                    for g in range(G):
                        update(CYCLES * n + c, g)

            def rope_and_split(b, f, sw, sw_in, parts, k):
                n = 2 * b + k
                pool.wait_ge(s("q_done" if k == 0 else "k_done"), b + 1)
                nc.gpsimd.tensor_tensor(ra[:], f[:], cosb[:], ALU.mult).then_inc(s("rope_a"), 1)
                pool.wait_ge(s(sw_in), SWAP * (b + 1))
                nc.gpsimd.tensor_tensor(rb[:], sw[:], sinb[:], ALU.mult).then_inc(s("rope_b"), 1)
                pool.wait_ge(s("rope_a"), n + 1)
                pool.wait_ge(s("rope_b"), n + 1)
                nc.gpsimd.tensor_tensor(rc[:], ra[:], rb[:], ALU.add).then_inc(s("rope_c"), 1)
                for half in range(2):
                    waits_for(pool, s(f"fill{half}"), FILL * b)
                nc.gpsimd.tensor_tensor(parts[:, 0], ra[:], rb[:], ALU.add).then_inc(s("part1"), 1)
                pool.wait_ge(s("rope_c"), n + 1)
                pool.wait_ge(s("part1"), n + 1)
                nc.gpsimd.tensor_tensor(rd[:], rc[:], parts[:, 0], ALU.subtract).then_inc(s("res1"), 1)
                nc.gpsimd.tensor_tensor(parts[:, 1], rc[:], parts[:, 0], ALU.subtract).then_inc(s("part2"), 1)
                pool.wait_ge(s("res1"), n + 1)
                pool.wait_ge(s("part2"), n + 1)
                nc.gpsimd.tensor_tensor(parts[:, 2], rd[:], parts[:, 1], ALU.subtract).then_inc(s("parts_ready"), 1)

            def iteration(i, q, first, last):
                if last <= B - 3:
                    invert(G + i + 2, slice(q, q + 1))
                    rope_and_split(i + 2, qf, qsw, "qsw_in", qp, 0)
                    rope_and_split(i + 2, kf, ksw, "ksw_in", kp, 1)

            pool.wait_ge(s("half_ready"), 1)
            feed_forward(0)
            pool.wait_ge(s("cst_in"), 32)
            pipeline(pool, iteration)
            feed_forward(1)

        @block.vector
        def _(dve):
            nc.vector.memset(w3s[:], 0.0)
            nc.vector.memset(w4s[:], 0.0).then_inc(s("setup_dve"), 1)
            nc.vector.memset(ones[:], 1.0)
            nc.vector.memset(vst[:].rearrange("p q t h c -> p (q t h c)"), 0.0).then_inc(s("setup_dve"), 1)
            dve.wait_ge(s("setup_dve"), 2)
            nc.vector.memset(vst[:].rearrange("p q t h c -> p (q t h) c")[:, :, DH:DH + 1], 1.0)\
                .then_inc(s("setup_dve"), 1)
            dve.wait_ge(s("ident_in"), 16)
            nc.vector.tensor_copy(ident_bf[:], ident[:]).then_inc(s("ident_ready"), 1)

            def token_stats(call, batches, slots):
                for src, k in zip(batches, range(slots.start, slots.stop)):
                    for t in range(T):
                        last = nc.vector.bn_stats(stats[:, k, t], src[:, t])
                last.then_inc(s("ln_stats"), 1)

            def token_variance(call, slots):
                for k in range(slots.start, slots.stop):
                    for t in range(T):
                        last = nc.vector.bn_aggr(mv[:, k, t], stats[:, k, t])
                last.then_inc(s("ln_mv"), 1)
                dve.wait_ge(s("ln_mv"), call + 1)
                nc.vector.tensor_scalar(var[:, slots], mv[:, slots, :, 1], EPS, None, ALU.add)\
                    .then_inc(s("ln_var"), 1)

            def normalise_tokens(src, dst, slot, ready):
                for t in range(T):
                    last = nc.vector.tensor_scalar(dst[:, t], src[:, t], mv[:, slot, t, 0:1], rstd[:, slot, t:t + 1],
                                                   ALU.subtract, ALU.mult)
                last.then_inc(ready, 1)

            def feed_forward(n):
                for g in range(G):
                    if n == 0:
                        dve.wait_ge(s(f"x_in{g}"), 16)
                    call = (G + B) * n + g
                    token_stats(call, [xs[:, b] for b in range(4 * g, 4 * g + 4)], slice(4 * g, 4 * g + 4))
                    dve.wait_ge(s("ln_stats"), call + 1)
                    token_variance(call, slice(4 * g, 4 * g + 4))
                for g in range(G):
                    dve.wait_ge(s("ln_rstd"), (G + B) * n + g + 1)
                    for b in range(4 * g, 4 * g + 4):
                        normalise_tokens(xs[:, b], st[:, b], b, s("ln_out"))
                if n == 0:
                    dve.wait_ge(s("wc_in"), 16 * WC_DMAS)
                    nc.vector.tensor_scalar(ar_tf[:], ar[:], TF_SHARE, None, ALU.mult)
                    nc.vector.tensor_scalar(ar_gf[:], ar[:], GF_SHARE, None, ALU.mult)
                    nc.vector.tensor_scalar(b4h[:], b4s[:], 0.5, None, ALU.mult)
                    nc.vector.tensor_scalar(gb3h[:], gb3s[:], 0.5, None, ALU.mult)
                    nc.vector.tensor_copy(g3r[:], g3s[:].to_broadcast([32, P])).then_inc(s("halves"), 1)
                    dve.wait_ge(s("halves"), 1)
                dve.wait_ge(s("gth_done"), n + 1)
                nc.vector.tensor_scalar(s0[:], gth[:], ar_gf[:], BASE_COUPLING, ALU.mult, ALU.add)\
                    .then_inc(s("s0_ready"), 1)
                dve.wait_ge(s("s0_ready"), n + 1)
                for g in range(G):
                    update(CYCLES * n, n, g)
                with dve.Fori(1, CYCLES) as c:
                    for g in range(G):
                        update(CYCLES * n + c, n, g)
                for b in range(B):
                    g, k = b // 4, b % 4
                    if k < 3:
                        dve.wait_ge(s("upd_dve", g), 3 * CYCLES * (n + 1) - 2 + k)
                    else:
                        dve.wait_ge(s("upd_pool", g), CYCLES * (n + 1))
                    nc.vector.scalar_tensor_tensor(
                        xs[:, b].rearrange("p t d -> p (t d)"), st[:, b].rearrange("p t d -> p (t d)"), 0.5,
                        xs[:, b].rearrange("p t d -> p (t d)"), ALU.mult, ALU.add).then_inc(s("x_new"), 1)

            def update(it, n, g):
                dve.wait_ge(s("th_done", g), it + 1)
                waits_for(dve, s("upd_pool", g), it)
                nc.vector.scalar_tensor_tensor(
                    cs[:, g, 0].rearrange("p (b t) -> p b t", b=4), th[:, g], ar_tf[:],
                    s0[:, 4 * g:4 * g + 4].unsqueeze(2).to_broadcast([P, 4, T]), ALU.mult, ALU.add)\
                    .then_inc(s("cs0", g), 1)
                dve.wait_ge(s("cs0", g), it + 1)
                nc.vector.tensor_copy(cs[:, g, 2], cs[:, g, 0])
                nc.vector.tensor_scalar(cs[:, g, 1], cs[:, g, 0], -1.0, None, ALU.mult).then_inc(s("cs_ready", g), 1)
                dve.wait_ge(s("cs_ready", g), it + 1)
                for k in range(3):
                    b = 4 * g + k
                    for a in range(2):
                        last = nc.vector.tensor_tensor(
                            tmp[:, g, k, :, 64 * a:64 * a + 64].rearrange("p t (u d) -> p t u d", u=2),
                            st[:, b, :, 64 - 64 * a:128 - 64 * a].rearrange("p t (u d) -> p t u d", u=2),
                            coupling(g, slice(T * k, T * k + T), a), ALU.mult)
                    last.then_inc(s("mul_done", g), 1)
                for k in range(3):
                    dve.wait_ge(s("mul_done", g), 3 * it + k + 1)
                    nc.vector.tensor_tensor(st[:, 4 * g + k], st[:, 4 * g + k], tmp[:, g, k], ALU.add)\
                        .then_inc(s("upd_dve", g), 1)

            def row_max(i, u, lt):
                n = (i + 1) * H * T + u * T + lt
                dve.wait_ge(s("s_ready"), n + 1)
                half, hl = u // HALF, u % HALF
                nc.vector.tensor_reduce(nmax[:, half, lt, hl % 2, hl // 2:hl // 2 + 1], ps[:, 4 + lt % 2, :],
                                        AX_X, ALU.max, negate=True).then_inc(s("s_used"), 1)

            def split_max(b, half):
                n = 2 * b + half
                dve.wait_ge(s("s_used"), b * H * T + (half + 1) * HALF * T)
                waits_for(dve, s("maxT_ready"), n)
                m = nmax[:, half]
                nc.vector.tensor_copy(nparts[:, :, :, 0], m).then_inc(s("n1"), 1)
                dve.wait_ge(s("n1"), n + 1)
                nc.vector.tensor_tensor(nres[:], m, nparts[:, :, :, 0], ALU.subtract).then_inc(s("nr1"), 1)
                dve.wait_ge(s("nr1"), n + 1)
                nc.vector.tensor_copy(nparts[:, :, :, 1], nres[:]).then_inc(s("n2"), 1)
                dve.wait_ge(s("n2"), n + 1)
                nc.vector.tensor_tensor(nparts[:, :, :, 2], nres[:], nparts[:, :, :, 1], ALU.subtract)\
                    .then_inc(s("n3"), 1)

            def normalise(i, lt):
                n = (i - 1) * T + lt
                dve.wait_ge(s("oT_ready"), n + 1)
                o = ps[:, 7, :].rearrange("p (h c) -> p h c", c=VC)
                nc.vector.reciprocal(rden[:, lt, :], o[:, :, DH]).then_inc(s("oT_rden"), 1)
                dve.wait_ge(s("oT_rden"), n + 1)
                waits_for(dve, s("onT_ready"), i - 1)
                nc.vector.tensor_tensor(on[:, lt].rearrange("p (h d) -> p h d", d=DH), o[:, :, 0:DH],
                                        rden[:, lt].unsqueeze(2).to_broadcast([P, H, DH]), ALU.mult)\
                    .then_inc(s("oT_used"), 1)

            def residual(i):
                dve.wait_ge(s("proj_ready"), i)
                nc.vector.tensor_tensor(batch_of(xs, i - 1), ps[:, 7, :], batch_of(xs, i - 1), ALU.add)\
                    .then_inc(s("proj_done"), 1)

            def batch_of(v, b):
                if isinstance(b, int):
                    return v[:, b].rearrange("p t d -> p (t d)")
                return v[:].rearrange("p b t d -> p (b t d)")[:, bass.ds(b * (T * D), T * D)]

            def iteration(i, q, first, last):
                for u in range(H):
                    if u < 2 and last <= B - 3:
                        b = i + 2
                        tokens = batch_of(xs, b).rearrange("p (t d) -> p t d", t=T)
                        if u == 0:
                            token_stats(G + b, [tokens], slice(q, q + 1))
                            dve.wait_ge(s("ln_stats"), G + b + 1)
                        else:
                            dve.wait_ge(s("ln_rstd"), G + b + 1)
                            waits_for(dve, s("xT_ready"), b - 1)
                            normalise_tokens(tokens, xn[:, q], q, s("xn_ready"))
                    if u == 2 and first >= 0 and last <= B - 1:
                        split_max(i, 1)
                    if u == HALF + 1 and first >= -1 and last <= B - 2:
                        split_max(i + 1, 0)
                    if first >= -1 and last <= B - 2:
                        for lt in range(T):
                            row_max(i, u, lt)
                    if u == 0 and last <= B - 3:
                        token_variance(G + i + 2, slice(q, q + 1))
                    if first >= 1 and 6 <= u < 6 + T:
                        normalise(i, u - 6)
                    if first >= 1 and u == 12:
                        residual(i)

            feed_forward(0)
            dve.wait_ge(s("x_new"), B)
            pipeline(dve, iteration)
            dve.wait_ge(s("proj_done"), B)
            feed_forward(1)

        @block.scalar
        def _(act):
            def evacuate(dst, src):
                return nc.scalar.activation(dst, src, ACT.Copy)

            def turned(it, g):
                for k in range(4):
                    act.wait_ge(s("T_ready", g), 4 * it + k + 1)
                    evacuate(xT[:, g, k], ps[:, 4 * g + k, :]).then_inc(s("T_copied", g), 1)

            def gelu1(it, g, ks):
                for k in ks:
                    act.wait_ge(s("L1_ready", g), 4 * it + k + 1)
                    nc.scalar.activation(h1[:, g, k], ps[:, 4 * g + k, :], ACT.Gelu, bias=b1s[:])\
                        .then_inc(s("h1_done", g), 1)

            def gelu2(it, g):
                for k in range(2):
                    act.wait_ge(s("L2_ready", g), 2 * it + k + 1)
                    nc.scalar.activation(h2[:, g, k], ps[:, 4 * g + k, :], ACT.Gelu, bias=b2s[:])\
                        .then_inc(s("h2_done", g), 1)

            def gelu3_tanh(it, g):
                act.wait_ge(s("L3_ready", g), it + 1)
                nc.scalar.activation(h3[:, g], ps[:, 4 * g + 2, :], ACT.Gelu, bias=b3s[:]).then_inc(s("h3_done", g), 1)
                act.wait_ge(s("L4_ready", g), it + 1)
                nc.scalar.activation(th[:, g].rearrange("p b t -> p t b"),
                                     ps[:, 4 * g + 3, 0:4 * T].rearrange("p (t b) -> p t b", b=4),
                                     ACT.Tanh, bias=b4h[:], scale=0.5).then_inc(s("th_done", g), 1)

            def feed_forward(n):
                act.wait_ge(s("gm_ready"), n + 1)
                nc.scalar.activation(gm[:], ps[:, 7, 0:B], ACT.Copy, scale=1.0 / S).then_inc(s("gm_copied"), 1)
                act.wait_ge(s("gh1_ready"), n + 1)
                nc.scalar.activation(gh1[:], ps[0:64, 6, 0:B], ACT.Gelu, bias=gb1s[:]).then_inc(s("gh1_done"), 1)
                act.wait_ge(s("gh2_ready"), n + 1)
                nc.scalar.activation(gh2[:], ps[0:32, 5, 0:B], ACT.Gelu, bias=gb2s[:]).then_inc(s("gh2_done"), 1)
                act.wait_ge(s("gth_ready"), n + 1)
                act.wait_ge(s("halves"), 1)
                nc.scalar.activation(gth[:], ps[:, 4, 0:B], ACT.Tanh, bias=gb3h[:], scale=0.5)\
                    .then_inc(s("gth_done"), 1)
                turned(CYCLES * n, 0)

                def cycle(it, more):
                    gelu1(it, 0, range(4))
                    turned(it, 1)
                    gelu2(it, 0)
                    gelu1(it, 1, (0, 1))
                    gelu3_tanh(it, 0)
                    gelu1(it, 1, (2, 3))
                    gelu2(it, 1)
                    if more:
                        turned(it + 1, 0)
                    gelu3_tanh(it, 1)

                with act.Fori(0, CYCLES - 1) as c:
                    cycle(CYCLES * n + c, True)
                cycle(CYCLES * n + CYCLES - 1, False)

            def exps(i, u):
                for k in range(2):
                    n = (i * H + u) * 2 + k
                    act.wait_ge(s("st_ready"), n + 1)
                    if k == 0 and u % 4 == 0:
                        waits_for(act, s("pv_ready"), 4 * i + u // 4 - 1)
                    nc.scalar.activation(probs[:, u % 8, 2 * S * k:2 * S * (k + 1)],
                                         ps[:, 2 * k:2 * k + 2, :].rearrange("p a c -> p (a c)"),
                                         ACT.Exp, scale=SCALE).then_inc(s("exp_done"), 1)

            def take_pv(i, q, u):
                g = (u - 8) // 4
                b = i if g >= 0 else i - 1
                g = g % 4
                act.wait_ge(s("pv_ready"), 4 * b + g + 1)
                waits_for(act, s("oT_ready"), T * (b - (g == 0)))
                evacuate(output_T(g, (q if b is i else 1 - q)), ps[:, 6, :]).then_inc(s("pv_used"), 1)

            def iteration(i, q, first, last):
                for u in range(H):
                    if first >= 0 and last <= B - 1:
                        exps(i, u)
                    if last <= B - 3:
                        b = i + 2
                        if u == 1:
                            act.wait_ge(s("xT_ready"), b + 1)
                            evacuate(xnT[:, q], ps[:, 7, :]).then_inc(s("xnT_done"), 1)
                        if u == 2:
                            act.wait_ge(s("q_ready"), b + 1)
                            waits_for(act, s("rope_b"), 2 * b - 1)
                            waits_for(act, s("qsw_in"), SWAP * b)
                            evacuate(qf[:], ps[:, 7, :]).then_inc(s("q_done"), 1)
                        if u == 4:
                            act.wait_ge(s("k_ready"), b + 1)
                            waits_for(act, s("rope_b"), 2 * b)
                            waits_for(act, s("ksw_in"), SWAP * b)
                            evacuate(kf[:], ps[:, 7, :]).then_inc(s("k_done"), 1)
                    if u == 3 and first >= 0 and last <= B - 1:
                        take_max(i, 1)
                    if u == 10 and first >= -1 and last <= B - 2:
                        take_max(i + 1, 0)
                    if u == 5 and first >= -1 and last <= B - 2:
                        act.wait_ge(s("v_ready"), i + 2)
                        evacuate(vst[:, 1 - q, :, :, 0:DH].rearrange("p t h d -> p (t h) d"),
                                 ps[:, 7, :].rearrange("p (a d) -> p a d", d=DH)).then_inc(s("v_done"), 1)
                    if u == 11 and first >= 1:
                        act.wait_ge(s("onT_ready"), i)
                        waits_for(act, s("proj_ready"), i - 1)
                        evacuate(onT, ps[:, 7, :]).then_inc(s("onT_done"), 1)
                    if u % 4 == 3:
                        if (u > 3 and first >= 0 and last <= B - 1) or (u == 3 and first >= 1):
                            take_pv(i, q, u + 1)

            def take_max(b, half):
                n = 2 * b + half
                act.wait_ge(s("maxT_ready"), n + 1)
                waits_for(act, s(f"mrow_out{1 - half}"), 32 * (b + half))
                evacuate(mrow[:], ps[0:6 * PAIRS, 7, 0:S // 2].bitcast(BF16)).then_inc(s("maxT_done"), 1)

            act.wait_ge(s("wT_ready"), 1)
            evacuate(wT[:].rearrange("p a c -> p (a c)"), ps[:, 7, :]).then_inc(s("wT_copied"), 1)
            feed_forward(0)
            pipeline(act, iteration)
            feed_forward(1)

        @block.tensor
        def _(pe):
            def turn(it, n, g, k, first):
                if first:
                    pe.wait_ge(s("ln_out"), B * n + 4 * g + k + 1)
                elif k < 3:
                    pe.wait_ge(s("upd_dve", g), 3 * it - 2 + k)
                else:
                    pe.wait_ge(s("upd_pool", g), it)
                for t in range(T):
                    last = nc.tensor.transpose(ps[:, 4 * g + k, P * t:P * t + P], st[:, 4 * g + k, t], ident[:])
                last.then_inc(s("T_ready", g), 1)

            def layer1(it, g, ks):
                for k in ks:
                    pe.wait_ge(s("T_copied", g), 4 * it + k + 1)
                    nc.tensor.matmul(ps[:, 4 * g + k, :], w1s[:], xT[:, g, k], start=True, stop=True)\
                        .then_inc(s("L1_ready", g), 1)

            def layer2(it, g):
                for pr in range(2):
                    pe.wait_ge(s("h1_done", g), 4 * it + 2 * pr + 2)
                    for k in range(2):
                        last = nc.tensor.matmul(ps[64 * k:64 * k + 64, 4 * g + pr, :], w2s[:], h1[:, g, 2 * pr + k],
                                                start=True, stop=True)
                    last.then_inc(s("L2_ready", g), 1)

            def layer34(it, g):
                pe.wait_ge(s("h2_done", g), 2 * it + 2)
                for pr in range(2):
                    last = nc.tensor.matmul(ps[64 * pr:64 * pr + 64, 4 * g + 2, :], w3s[:], h2[:, g, pr],
                                            start=True, stop=True)
                last.then_inc(s("L3_ready", g), 1)
                pe.wait_ge(s("h3_done", g), it + 1)
                for t in range(T):
                    last = nc.tensor.matmul(ps[:, 4 * g + 3, 4 * t:4 * t + 4], h3[:, g, P * t:P * t + P], w4s[:],
                                            start=True, stop=True)
                last.then_inc(s("L4_ready", g), 1)

            def feed_forward(n):
                for b in range(B):
                    pe.wait_ge(s("ln_out"), B * n + b + 1)
                    for t in range(T):
                        last = nc.tensor.matmul(ps[:, 7, b:b + 1], st[:, b, t], ones[:],
                                                start=(t == 0), stop=(t == T - 1))
                last.then_inc(s("gm_ready"), 1)
                for k in range(4):
                    turn(CYCLES * n, n, 0, k, True)
                pe.wait_ge(s("gm_copied"), n + 1)
                nc.tensor.matmul(ps[0:64, 6, 0:B], g1s[:], gm[:], start=True, stop=True).then_inc(s("gh1_ready"), 1)
                pe.wait_ge(s("gh1_done"), n + 1)
                nc.tensor.matmul(ps[0:32, 5, 0:B], g2s[:], gh1[:], start=True, stop=True).then_inc(s("gh2_ready"), 1)
                pe.wait_ge(s("gh2_done"), n + 1)
                pe.wait_ge(s("halves"), 1)
                nc.tensor.matmul(ps[:, 4, 0:B], g3r[:], gh2[:], start=True, stop=True).then_inc(s("gth_ready"), 1)

                def cycle(it, first, more):
                    layer1(it, 0, range(4))
                    if first:
                        pe.wait_ge(s("gth_done"), n + 1)
                    for k in range(4):
                        turn(it, n, 1, k, first)
                    layer2(it, 0)
                    layer1(it, 1, (0, 1))
                    layer34(it, 0)
                    layer1(it, 1, (2, 3))
                    layer2(it, 1)
                    if more:
                        for k in range(4):
                            turn(it + 1, n, 0, k, False)
                    layer34(it, 1)

                cycle(CYCLES * n, True, True)
                with pe.Fori(1, CYCLES - 1) as c:
                    cycle(CYCLES * n + c, False, True)
                cycle(CYCLES * n + CYCLES - 1, False, False)

            def scores_T(i, q, u, k):
                n = (i * H + u) * 2 + k
                if u % HALF == 0 and k == 0:
                    pe.wait_ge(s(f"mrow_out{u // HALF}"), 32 * i + 32)
                waits_for(pe, s("exp_done"), n - 1)
                for mt in (2 * k, 2 * k + 1):
                    last = nc.tensor.matmul(ps[:, mt, :], kst[:, q, u, P * mt:P * mt + P], qst[:, q, u // 2, :],
                                            start=True, stop=True)
                last.then_inc(s("st_ready"), 1)

            def scores(i, q, u, lt):
                n = (i + 1) * H * T + u * T + lt
                if u % HALF == 0 and lt == 0:
                    pe.wait_ge(s(f"fill{u // HALF}"), FILL * (i + 2))
                waits_for(pe, s("s_used"), n - 1)
                nc.tensor.matmul(ps[:, 4 + lt % 2, :], qst[:, 1 - q, u // 2, P * lt:P * lt + P], kst[:, 1 - q, u, :],
                                 start=True, stop=True).then_inc(s("s_ready"), 1)

            def products(i, q, u):
                g = u // 4 - 1
                b, qb = (i, q) if g >= 0 else (i - 1, 1 - q)
                g, mt = g % 4, u % 4
                if mt == 0:
                    pe.wait_ge(s("exp_done"), (4 * b + g + 1) * 8)
                    waits_for(pe, s("pv_used"), 4 * b + g)
                    if g == 0:
                        pe.wait_ge(s("v_done"), b + 1)
                for j in range(4):
                    h = 4 * g + j
                    last = nc.tensor.matmul(ps[32 * j:32 * j + 32, 6, :], vst[:, qb, mt, h, :],
                                            probs[:, h % 8, S * mt:S * mt + S], start=(mt == 0), stop=(mt == T - 1))
                if mt == T - 1:
                    last.then_inc(s("pv_ready"), 1)

            def project(b, w, ready, xq):
                nc.tensor.matmul(ps[:, 7, :], wT[:, w], xnT[:, xq], start=True, stop=True).then_inc(s(ready), 1)

            def turn_max(b, half):
                pe.wait_ge(s("n3"), 2 * b + half + 1)
                for t in range(T):
                    last = nc.tensor.transpose(ps[0:6 * PAIRS, 7, 0:S // 2].bitcast(BF16)[:, P * t:P * t + P],
                                               nparts[:, t].rearrange("p a k h -> p (a k h)"), ident_bf[:])
                last.then_inc(s("maxT_ready"), 1)

            def side_work(i, q, u, first, last_i):
                a_on = last_i <= B - 3
                c_on = first >= 1
                if u == 1 and a_on:
                    b = i + 2
                    waits_for(pe, s("proj_done"), i - 1)
                    waits_for(pe, s("maxT_done"), 2 * (i + 1) - 1)
                    waits_for(pe, s("v_done"), i + 1)
                    waits_for(pe, s("k_done"), i + 2)
                    pe.wait_ge(s("xn_ready"), b + 1)
                    for t in range(T):
                        last = nc.tensor.transpose(ps[:, 7, P * t:P * t + P], xn[:, q, t], ident[:])
                    last.then_inc(s("xT_ready"), 1)
                if u == 2 and a_on:
                    pe.wait_ge(s("xnT_done"), i + 3)
                    project(i + 2, 0, "q_ready", q)
                if u == 3 and first >= 0 and last_i <= B - 1:
                    waits_for(pe, s("q_done"), i + 3 if a_on else 0)
                    waits_for(pe, s("proj_done"), i - 1 if not a_on else 0)
                    turn_max(i, 1)
                if u == 4 and a_on:
                    waits_for(pe, s("maxT_done"), 2 * i + 2 if first >= 0 else 0)
                    pe.wait_ge(s("q_done"), i + 3)
                    project(i + 2, 1, "k_ready", q)
                if u == 5 and first >= -1 and last_i <= B - 2:
                    waits_for(pe, s("k_done"), i + 3 if a_on else 0)
                    waits_for(pe, s("maxT_done"), 2 * i + 2 if first >= 0 else 0)
                    for t in range(T):
                        last = nc.tensor.matmul(ps[:, 7, P * t:P * t + P], xnT[:, 1 - q, P * t:P * t + P], wT[:, 2],
                                                start=True, stop=True)
                    last.then_inc(s("v_ready"), 1)
                if c_on and 6 <= u < 6 + T:
                    lt = u - 6
                    if lt == 0:
                        pe.wait_ge(s("pv_used"), 4 * i)
                        waits_for(pe, s("proj_done"), i - 1)
                        waits_for(pe, s("v_done"), i + 2 if last_i <= B - 2 else 0)
                        waits_for(pe, s("maxT_done"), 2 * i + 2 if last_i <= B - 1 else 0)
                    waits_for(pe, s("oT_used"), T * (i - 1) + lt)
                    for g in range(4):
                        last = nc.tensor.transpose(ps[:, 7, P * g:P * g + P], output_T(g, 1 - q)[:, P * lt:P * lt + P], ident[:])
                    last.then_inc(s("oT_ready"), 1)
                if u == 10 and first >= -1 and last_i <= B - 2:
                    waits_for(pe, s("oT_used"), T * i if c_on else 0)
                    pe.wait_ge(s("v_done"), i + 2)
                    turn_max(i + 1, 0)
                if c_on and u == 11:
                    pe.wait_ge(s("oT_used"), T * i)
                    waits_for(pe, s("maxT_done"), 2 * i + 3 if last_i <= B - 2 else 0)
                    for t in range(T):
                        last = nc.tensor.transpose(ps[:, 7, P * t:P * t + P], on[:, t], ident[:])
                    last.then_inc(s("onT_ready"), 1)
                if c_on and u == 12:
                    pe.wait_ge(s("onT_done"), i)
                    for t in range(T):
                        last = nc.tensor.matmul(ps[:, 7, P * t:P * t + P], onT[:, P * t:P * t + P], wT[:, 3],
                                                start=True, stop=True)
                    last.then_inc(s("proj_ready"), 1)

            def iteration(i, q, first, last):
                for u in range(H):
                    st_on = first >= 0 and last <= B - 1
                    s_on = first >= -1 and last <= B - 2
                    pv_on = (u >= 4 and st_on) or (u < 4 and first >= 1)
                    if st_on:
                        scores_T(i, q, u, 0)
                    if s_on:
                        scores(i, q, u, 0)
                        scores(i, q, u, 1)
                    if pv_on:
                        products(i, q, u)
                    if st_on:
                        scores_T(i, q, u, 1)
                    if s_on:
                        scores(i, q, u, 2)
                        scores(i, q, u, 3)
                    side_work(i, q, u, first, last)

            pe.wait_ge(s("ident_in"), 16)
            pe.wait_ge(s("ident_ready"), 1)
            pe.wait_ge(s("setup_dve"), 3)
            pe.wait_ge(s("wc_in"), 16 * WC_DMAS)
            pe.wait_ge(s("w_in"), 16 * 9)
            for j in range(4):
                last = nc.tensor.transpose(ps[:, 7, P * j:P * j + P], wnat[:, j], ident[:])
            last.then_inc(s("wT_ready"), 1)
            pe.wait_ge(s("wT_copied"), 1)
            feed_forward(0)
            pe.wait_ge(s("x_new"), B)
            pe.wait_ge(s("ones_dma"), 16 * 4)
            pipeline(pe, iteration)
            pe.wait_ge(s("proj_done"), B)
            feed_forward(1)


_INS = ['L0_attn_x', 'L0_attn_w_qkv', 'L0_attn_w_out',
        'L0_ffn_cn_w1', 'L0_ffn_cn_b1', 'L0_ffn_cn_w2', 'L0_ffn_cn_b2',
        'L0_ffn_cn_w3', 'L0_ffn_cn_b3', 'L0_ffn_cn_w4', 'L0_ffn_cn_b4',
        'L0_ffn_gc_w1', 'L0_ffn_gc_b1', 'L0_ffn_gc_w2', 'L0_ffn_gc_b2', 'L0_ffn_gc_w3', 'L0_ffn_gc_b3',
        'L0_ffn_adaptive_range']


def shape_constants(S, D, H):
    import numpy as np
    dh = D // H
    half = dh // 2
    inv_freq = (np.float32(1.0) / np.float32(10000.0) ** (np.arange(half, dtype=np.float32) / np.float32(half)))
    ang = np.arange(S, dtype=np.float32)[:, None] * inv_freq.astype(np.float32)[None, :]
    cos, sin = np.cos(ang).astype(np.float32).T, np.sin(ang).astype(np.float32).T
    cos = np.tile(np.repeat(np.concatenate([cos, cos]), H // 4, axis=0), (4, 1))
    sin = np.tile(np.repeat(np.concatenate([-sin, sin]), H // 4, axis=0), (4, 1))
    return (np.ascontiguousarray(cos), np.ascontiguousarray(sin), np.eye(128, dtype=np.float32))


def kernel(**inputs):
    import numpy as _np
    import concourse.bacc as _bacc
    from concourse import mybir as _mybir
    from concourse.bass_utils import run_bass_kernel_spmd as _run

    nc = _bacc.Bacc("TRN2", target_bir_lowering=False, num_devices=1)
    arrays, args = {}, []

    def give(name, a):
        arrays[name] = a
        return nc.dram_tensor(name, a.shape, _mybir.dt.from_np(a.dtype), kind="ExternalInput").ap()

    for name in _INS:
        args.append(give(f"in_{name}_dram", _np.ascontiguousarray(inputs[name])))
    B, S, D = inputs['L0_attn_x'].shape
    tables = [give(f"in_{n}_dram", a) for n, a in zip(("cos", "sin", "ident"), shape_constants(S, D, 16))]
    out = nc.dram_tensor("out_0_dram", (B, S, D), _mybir.dt.float32, kind="ExternalOutput").ap()
    macaron_kernel(nc, args[0], args[1], args[2], args[3:11], args[11:17], args[17], *tables, out)
    r = _run(nc, [arrays], core_ids=[0])
    return r.results[0]["out_0_dram"]
```

```python
from contextlib import ExitStack

import concourse.bass as bass
from concourse import mybir

P = 128
F32 = mybir.dt.float32
BF16 = mybir.dt.bfloat16
ALU = mybir.AluOpType
ACT = mybir.ActivationFunctionType
AX_X = mybir.AxisListType.X

EPS = 1e-5
BASE_COUPLING = 0.1
GF_SHARE, TF_SHARE = 0.7, 0.3
CYCLES = 3

Q_PARTS = [0, 0, 0, 1, 1, 2]
K_PARTS = [0, 1, 2, 0, 1, 0]
TERMS = len(Q_PARTS)


def macaron_kernel(nc, x, w_qkv, w_out, cn, gc, adaptive_range, cos_t, sin_t, ident_t, out):
    B, S, D = x.shape
    H, DH = 16, D // 16
    T = S // P
    HP = H // 2
    HALF = H // 2
    PAIRS = HALF // 2
    G = B // 4
    HEAD_ROWS = TERMS * DH
    MAX_ROW = 2 * HEAD_ROWS
    ROWS = MAX_ROW + 6
    SCALE = float(DH) ** -0.5
    VC = 32
    (w1, b1, w2, b2, w3, b3, w4, b4), (g1, gb1, g2, gb2, g3, gb3) = cn, gc

    with ExitStack() as ctx:
        def sb(name, shape, dt=F32):
            return ctx.enter_context(nc.sbuf_tensor(name, shape, dt))

        def sem(name):
            return ctx.enter_context(nc.semaphore(name))

        ps = ctx.enter_context(nc.psum_tensor("ps", [P, 8, 512], F32))

        xs = sb("xs", [P, B, T, D])
        st = sb("st", [P, B, T, D])
        ident = sb("ident", [P, P])
        ident_bf = sb("ident_bf", [P, P], BF16)
        cosb, sinb = sb("cosb", [P, S]), sb("sinb", [P, S])
        w1s, w2s, w3s = sb("w1s", [P, 128]), sb("w2s", [P, 64]), sb("w3s", [P, 64])
        w4s = sb("w4s", [P, 4])
        g1s, g2s, g3s, g3r = sb("g1s", [P, 64]), sb("g2s", [64, 32]), sb("g3s", [32, 1]), sb("g3r", [32, P])
        b1s, b2s, b3s, b4s = sb("b1s", [P, 1]), sb("b2s", [P, 1]), sb("b3s", [P, 1]), sb("b4s", [P, 1])
        gb1s, gb2s, gb3s = sb("gb1s", [64, 1]), sb("gb2s", [32, 1]), sb("gb3s", [P, 1])
        b4h, gb3h = sb("b4h", [P, 1]), sb("gb3h", [P, 1])
        ar, ar_tf, ar_gf = sb("ar", [P, 1]), sb("ar_tf", [P, 1]), sb("ar_gf", [P, 1])
        wT = sb("wT", [P, 4, D])
        stats, mv = sb("stats", [P, B, T, 6]), sb("mv", [P, B, T, 2])
        var, rstd, minus_half = sb("var", [P, B, T]), sb("rstd", [P, B, T]), sb("minus_half", [P, B, T])
        gm, gh1, gh2, gth = sb("gm", [P, B]), sb("gh1", [64, B]), sb("gh2", [32, B]), sb("gth", [P, B])
        s0 = sb("s0", [P, B])
        th = sb("th", [P, G, 4, T])
        cs = sb("cs", [P, G, 3, 4 * T])
        big = sb("big", [P, 8, T * S])
        by_group = big[:].rearrange("p (g j) (b s) -> p g j b s", g=G, b=4)
        xT, h1 = by_group[:, :, 0], by_group[:, :, 1]
        tmp = big[:].rearrange("p (g j) (b t d) -> p g j b t d", g=G, b=4, t=T)[:, :, 2]
        h2, h3 = by_group[:, :, 3, 0:2], by_group[:, :, 3, 2]
        wnat = big[:, 7, 3 * S:3 * S + 4 * D].rearrange("p (a d) -> p a d", a=4)
        probs = big
        xn = st[:, 0:2]
        ra, rb = st[:, 2].rearrange("p t d -> p (t d)"), st[:, 3].rearrange("p t d -> p (t d)")
        oT = st[:, 4:8].rearrange("p g t d -> p g (t d)")
        oT0 = sb("oT0", [P, S])
        on, onT = sb("on", [P, T, D]), sb("onT", [P, S])
        xnT = sb("xnT", [P, 2, S])
        qkf, qksw = sb("qkf", [P, 2, S]), sb("qksw", [P, 2, S])
        rc, rd = sb("rc", [P, S]), sb("rd", [P, S])
        parts = sb("parts", [P, 2, 3, S], BF16)
        qst = sb("qst", [ROWS, 2, HP, S], BF16)
        kst = sb("kst", [ROWS, 2, HP, 2, S], BF16)
        orow = sb("orow", [3, S], BF16)
        vst = sb("vst", [P, 2, T, H, VC])
        nmax = sb("nmax", [P, 2, T, 2, PAIRS])
        nres = sb("nres", [P, T, 2, PAIRS])
        nparts = sb("nparts", [P, T, 2, 3, PAIRS], BF16)
        mrow = sb("mrow", [6 * PAIRS, S], BF16)
        rden = sb("rden", [P, T, H])

        S_ = {}
        for name in (
            "ident_in half_ready ln_var x_in0 x_in1 x_in2 x_in3 w_in w1_in cst_in wc_in st_out setup_dve setup_pool ones_dma ident_ready halves "
            "wT_ready wT_copied ln_stats ln_mv ln_rstd ln_out x_new first_q "
            "xn_ready xT_ready xnT_done q_ready q_done k_ready k_done v_ready v_done swapped rope_a rope_b "
            "rope_c part1 res1 part2 parts_ready fill0 fill1 st_ready st_used s_ready s_used "
            "exp_done pv_ready pv_used pv_step n1 nr1 n2 n3 maxT_ready maxT_done mrow_out0 mrow_out1 "
            "oT_ready oT_rden oT_used on_done onT_ready onT_done proj_ready proj_done kept0 kept1"
        ).split():
            S_[name] = sem(name)
        for g in range(G):
            for name in "T_ready T_copied L1_ready h1_done L2_ready h2_done L3_ready h3_done L4_ready th_done cs0 cs1 cs_ready mul_done upd_dve mul_pool upd_pool gh1_ready gh1_done gh2_ready gh2_done gth_ready gth_done s0_ready half_added".split():
                S_[name, g] = sem(f"{name}_{g}")

        def s(name, g=None):
            return S_[name] if g is None else S_[name, g]

        x_dram = x.rearrange("b (t p) d -> p b t d", p=P)
        out_dram = out.rearrange("b (t p) d -> p b t d", p=P)
        col = lambda v: v.rearrange("(p a) -> p a", a=1)

        def waits_for(eng, semaphore, count):
            if not isinstance(count, int) or count > 0:
                eng.wait_ge(semaphore, count)

        block = ctx.enter_context(nc.Block())
        WC_DMAS = 21
        SWAP_ROWS = PAIRS * DH // 2
        SWAPPED = [(r + SWAP_ROWS) % (2 * SWAP_ROWS) for r in range(2 * SWAP_ROWS)]
        LN_CALLS = B // 2
        FILL = 16 * 2 * 2 * TERMS

        def pipeline(eng, iteration):
            for i in (-1, 0, 1):
                iteration(i, i % 2, i, i)
            with eng.Fori(1, B // 2 - 1) as j:
                for q in range(2):
                    iteration(2 * j + q, q, 2, B - 3)
            iteration(B - 2, (B - 2) % 2, B - 2, B - 2)

        def output_T(g, q):
            return oT0[:] if g == 0 and q else oT[:, g]

        def global_out(g, step):
            return ps[:, (g + step) % 2, 0:4]

        def coupling(g, k, a):
            v = cs[:, g, a:a + 2, k]
            return v.rearrange("p u t -> p t u").unsqueeze(3).to_broadcast([P, k.stop - k.start, 2, 32])

        @block.sync
        def _(sp):
            def load_x(pair):
                sp.dma_start(xs[:, 2 * pair:2 * pair + 2], x_dram[:, 2 * pair:2 * pair + 2])\
                    .then_inc(s(f"x_in{pair}"), 16)

            load_x(0)
            sp.dma_start(ident[:], ident_t).then_inc(s("ident_in"), 16)
            sp.dma_start(w1s[:], w1).then_inc(s("w1_in"), 16)
            sp.dma_start(b1s[:], col(b1)).then_inc(s("w1_in"), 16)
            load_x(1)
            sp.wait_ge(s("setup_dve"), 1)
            jobs = [(w2s[:], w2), (g1s[:], g1), (g2s[:], g2), (g3s[:], g3),
                    (gb1s[:], col(gb1)), (gb2s[:], col(gb2)),
                    (b4s[:], b4.partition_broadcast(P)), (gb3s[:], gb3.partition_broadcast(P)),
                    (ar[:], adaptive_range.partition_broadcast(P))]
            jobs += [(b2s[64 * i:64 * i + 64], col(b2)) for i in range(2)]
            jobs += [(b3s[32 * i:32 * i + 32], col(b3)) for i in range(4)]
            jobs += [(w3s[64 * i:64 * i + 64, 32 * i:32 * i + 32], w3) for i in range(2)]
            jobs += [(w4s[32 * i:32 * i + 32, i:i + 1], w4) for i in range(4)]
            assert len(jobs) == WC_DMAS
            for dst, src in jobs:
                sp.dma_start(dst, src).then_inc(s("wc_in"), 16)
            load_x(2)
            load_x(3)
            sp.dma_start(wnat[:, 3], w_out).then_inc(s("w_in"), 16)
            for j in range(2):
                src = w_qkv[j * D:(j + 1) * D].rearrange("(f hp par d) c -> par f d hp c", f=2, par=2, d=DH)
                for par in range(2):
                    for f in range(2):
                        r = 64 * par + 32 * f
                        sp.dma_start(wnat[r:r + 32, j], src[par, f]).then_inc(s("w_in"), 16)
            sp.dma_start(wnat[:, 2], w_qkv[2 * D:3 * D]).then_inc(s("w_in"), 16)
            sp.dma_start(cosb[:], cos_t).then_inc(s("cst_in"), 16)
            sp.dma_start(sinb[:], sin_t).then_inc(s("cst_in"), 16)
            sp.wait_ge(s("setup_pool"), 1)
            for q in range(2):
                for par in range(2):
                    r = MAX_ROW + 3 * par
                    sp.dma_start(kst[r:r + 3, q, :, par, :], orow[:].unsqueeze(1).to_broadcast([3, HP, S]))\
                        .then_inc(s("ones_dma"), 16)

            def stack_part(q, half, k, part):
                pairs = slice(PAIRS * half, PAIRS * (half + 1))
                for par in range(2):
                    for t in range(TERMS):
                        if (Q_PARTS, K_PARTS)[k][t] == part:
                            r = HEAD_ROWS * par + t * DH
                            p0 = 64 * par + PAIRS * DH * half
                            dst = kst[r:r + DH, q, pairs, par, :] if k else qst[r:r + DH, q, pairs, :]
                            sp.dma_start(dst, parts[p0:p0 + PAIRS * DH, k, part, :]).then_inc(s(f"fill{half}"), 16)

            def fill(b, q, half):
                if half == 0:
                    sp.wait_ge(s("parts_ready"), 2 * b + 1)
                elif not isinstance(b, int) or b >= 2:
                    sp.wait_ge(s("st_ready"), T * H * (b - 1))
                for k in range(2):
                    for part in range(3):
                        stack_part(q, half, k, part)

            def max_rows(b, q, half):
                sp.wait_ge(s("maxT_done"), 2 * b + half + 1)
                sp.dma_start(qst[MAX_ROW:ROWS, q, PAIRS * half:PAIRS * (half + 1), :], mrow[:])\
                    .then_inc(s(f"mrow_out{half}"), 16)

            def iteration(i, q, first, last):
                if first >= 0 and last <= B - 2:
                    fill(i + 1, 1 - q, 1)
                if first >= 0:
                    max_rows(i, q, 1)
                if first >= 0 and last <= B - 2:
                    max_rows(i + 1, 1 - q, 0)
                if first >= 0 and last <= B - 3:
                    fill(i + 2, q, 0)

            for part, done in enumerate((4, 6, 7)):
                sp.wait_ge(s("first_q"), done)
                stack_part(0, 0, 0, part)
            for part, done in enumerate(("part1", "part2", "parts_ready")):
                sp.wait_ge(s(done), 1)
                stack_part(0, 0, 1, part)
            fill(0, 0, 1)
            fill(1, 1, 0)
            max_rows(0, 0, 0)
            pipeline(sp, iteration)
            iteration(B - 1, 1, B - 1, B - 1)

            for b in range(B):
                sp.wait_ge(s("x_new"), B + b + 1)
                sp.dma_start(out_dram[:, b], xs[:, b]).then_inc(s("st_out"), 16)
            sp.wait_ge(s("st_out"), 16 * B)

        @block.gpsimd
        def _(pool):
            nc.gpsimd.memset(minus_half[:], -0.5).then_inc(s("half_ready"), 1)

            def multiply(it, g):
                pool.wait_ge(s("cs_ready", g), it + 1)
                b, k = 4 * g + 3, slice(3 * T, 4 * T)
                for a in range(2):
                    last = nc.gpsimd.tensor_tensor(
                        tmp[:, g, 3, :, 64 * a:64 * a + 64].rearrange("p t (u d) -> p t u d", u=2),
                        st[:, b, :, 64 - 64 * a:128 - 64 * a].rearrange("p t (u d) -> p t u d", u=2),
                        coupling(g, k, a), ALU.mult)
                last.then_inc(s("mul_pool", g), 1)

            def update(it, g):
                multiply(it, g)
                pool.wait_ge(s("mul_pool", g), it + 1)
                nc.gpsimd.tensor_tensor(st[:, 4 * g + 3], st[:, 4 * g + 3], tmp[:, g, 3], ALU.add)\
                    .then_inc(s("upd_pool", g), 1)

            def invert(call, slots):
                pool.wait_ge(s("ln_var"), call + 1)
                nc.gpsimd.tensor_tensor(rstd[:, slots], var[:, slots], minus_half[:, slots], ALU.pow)\
                    .then_inc(s("ln_rstd"), 1)

            def cycles(n):
                with pool.Fori(0, CYCLES - 1) as c:
                    for g in range(G):
                        update(CYCLES * n + c, g)

            def rope_and_split(b, k):
                n = 2 * b + k - 1
                pool.wait_ge(s("q_done" if k == 0 else "k_done"), b + 1)
                nc.gpsimd.tensor_tensor(ra[:], qkf[:, k], cosb[:], ALU.mult).then_inc(s("rope_a"), 1)
                pool.wait_ge(s("swapped"), n + 2)
                nc.gpsimd.tensor_tensor(rb[:], qksw[:, k], sinb[:], ALU.mult).then_inc(s("rope_b"), 1)
                pool.wait_ge(s("rope_a"), n + 1)
                pool.wait_ge(s("rope_b"), n + 1)
                nc.gpsimd.tensor_tensor(rc[:], ra[:], rb[:], ALU.add).then_inc(s("rope_c"), 1)
                for half in range(2):
                    waits_for(pool, s(f"fill{half}"), FILL * b)
                nc.gpsimd.tensor_tensor(parts[:, k, 0], ra[:], rb[:], ALU.add).then_inc(s("part1"), 1)
                pool.wait_ge(s("rope_c"), n + 1)
                pool.wait_ge(s("part1"), n + 1)
                nc.gpsimd.tensor_tensor(rd[:], rc[:], parts[:, k, 0], ALU.subtract).then_inc(s("res1"), 1)
                nc.gpsimd.tensor_tensor(parts[:, k, 1], rc[:], parts[:, k, 0], ALU.subtract).then_inc(s("part2"), 1)
                pool.wait_ge(s("res1"), n + 1)
                pool.wait_ge(s("part2"), n + 1)
                nc.gpsimd.tensor_tensor(parts[:, k, 2], rd[:], parts[:, k, 1], ALU.subtract)\
                    .then_inc(s("parts_ready"), 1)

            def iteration(i, q, first, last):
                if first >= 0 and last <= B - 3:
                    invert(LN_CALLS + i + 2, slice(q, q + 1))
                    rope_and_split(i + 2, 0)
                    rope_and_split(i + 2, 1)

            pool.wait_ge(s("half_ready"), 1)
            for pair in range(LN_CALLS):
                invert(pair, slice(2 * pair, 2 * pair + 2))
            nc.gpsimd.memset(orow[:], 1.0)
            nc.gpsimd.memset(kst[:].rearrange("p q h e c -> p (q h e c)").bitcast(F32), 0.0)\
                .then_inc(s("setup_pool"), 1)
            cycles(0)
            multiply(CYCLES - 1, 0)
            invert(LN_CALLS, slice(0, 1))
            pool.wait_ge(s("cst_in"), 32)
            rope_and_split(0, 1)
            invert(LN_CALLS + 1, slice(1, 2))
            multiply(CYCLES - 1, 1)
            rope_and_split(1, 0)
            rope_and_split(1, 1)
            pipeline(pool, iteration)
            for pair in range(LN_CALLS):
                invert(LN_CALLS + B + pair, slice(2 * pair, 2 * pair + 2))
            cycles(1)
            for g in range(G):
                multiply(2 * CYCLES - 1, g)

        @block.vector
        def _(dve):
            nc.vector.memset(w3s[:], 0.0)
            nc.vector.memset(w4s[:], 0.0).then_inc(s("setup_dve"), 1)
            nc.vector.memset(vst[:].rearrange("p q t h c -> p (q t h c)"), 0.0).then_inc(s("setup_dve"), 1)
            dve.wait_ge(s("setup_dve"), 2)
            nc.vector.memset(vst[:].rearrange("p q t h c -> p (q t h) c")[:, :, DH:DH + 1], 1.0)\
                .then_inc(s("setup_dve"), 1)

            def token_stats(call, batches, slots):
                for src, k in zip(batches, range(slots.start, slots.stop)):
                    for t in range(T):
                        last = nc.vector.bn_stats(stats[:, k, t], src[:, t])
                last.then_inc(s("ln_stats"), 1)

            def token_variance(call, slots):
                for k in range(slots.start, slots.stop):
                    for t in range(T):
                        last = nc.vector.bn_aggr(mv[:, k, t], stats[:, k, t])
                last.then_inc(s("ln_mv"), 1)
                dve.wait_ge(s("ln_mv"), call + 1)
                nc.vector.tensor_scalar(var[:, slots], mv[:, slots, :, 1], EPS, None, ALU.add)\
                    .then_inc(s("ln_var"), 1)

            def normalise_tokens(src, dst, slot, ready):
                for t in range(T):
                    last = nc.vector.tensor_scalar(dst[:, t], src[:, t], mv[:, slot, t, 0:1], rstd[:, slot, t:t + 1],
                                                   ALU.subtract, ALU.mult)
                last.then_inc(ready, 1)

            def pair_variance(n, pair):
                call, slots = (LN_CALLS + B) * n + pair, slice(2 * pair, 2 * pair + 2)
                if n == 0:
                    dve.wait_ge(s(f"x_in{pair}"), 16)
                token_stats(call, [xs[:, 2 * pair], xs[:, 2 * pair + 1]], slots)
                dve.wait_ge(s("ln_stats"), call + 1)
                token_variance(call, slots)

            def pair_normalise(n, pair):
                dve.wait_ge(s("ln_rstd"), (LN_CALLS + B) * n + pair + 1)
                for b in (2 * pair, 2 * pair + 1):
                    normalise_tokens(xs[:, b], st[:, b], b, s("ln_out"))

            def halves():
                dve.wait_ge(s("wc_in"), 16 * WC_DMAS)
                nc.vector.tensor_scalar(ar_tf[:], ar[:], TF_SHARE, None, ALU.mult)
                nc.vector.tensor_scalar(ar_gf[:], ar[:], GF_SHARE, None, ALU.mult)
                nc.vector.tensor_scalar(b4h[:], b4s[:], 0.5, None, ALU.mult)
                nc.vector.tensor_scalar(gb3h[:], gb3s[:], 0.5, None, ALU.mult)
                nc.vector.tensor_copy(g3r[:], g3s[:].to_broadcast([32, P])).then_inc(s("halves"), 1)

            def couple(it, g):
                dve.wait_ge(s("th_done", g), it + 1)
                waits_for(dve, s("mul_pool", g), it)
                nc.vector.scalar_tensor_tensor(
                    cs[:, g, 0].rearrange("p (b t) -> p b t", b=4), th[:, g], ar_tf[:],
                    s0[:, 4 * g:4 * g + 4].unsqueeze(2).to_broadcast([P, 4, T]), ALU.mult, ALU.add)\
                    .then_inc(s("cs0", g), 1)
                dve.wait_ge(s("cs0", g), it + 1)
                nc.vector.tensor_copy(cs[:, g, 2], cs[:, g, 0])
                nc.vector.tensor_scalar(cs[:, g, 1], cs[:, g, 0], -1.0, None, ALU.mult).then_inc(s("cs_ready", g), 1)
                dve.wait_ge(s("cs_ready", g), it + 1)

            def multiply(g, k):
                for a in range(2):
                    last = nc.vector.tensor_tensor(
                        tmp[:, g, k, :, 64 * a:64 * a + 64].rearrange("p t (u d) -> p t u d", u=2),
                        st[:, 4 * g + k, :, 64 - 64 * a:128 - 64 * a].rearrange("p t (u d) -> p t u d", u=2),
                        coupling(g, slice(T * k, T * k + T), a), ALU.mult)
                last.then_inc(s("mul_done", g), 1)

            def update(it, g):
                couple(it, g)
                for k in range(3):
                    multiply(g, k)
                for k in range(3):
                    dve.wait_ge(s("mul_done", g), 3 * it + k + 1)
                    nc.vector.tensor_tensor(st[:, 4 * g + k], st[:, 4 * g + k], tmp[:, g, k], ALU.add)\
                        .then_inc(s("upd_dve", g), 1)

            def add_half(v, b):
                x_b = xs[:, b].rearrange("p t d -> p (t d)")
                return nc.vector.scalar_tensor_tensor(x_b, v.rearrange("p t d -> p (t d)"), 0.5, x_b,
                                                      ALU.mult, ALU.add)

            def add_state(n, g):
                for k in range(4):
                    if k < 3:
                        dve.wait_ge(s("upd_dve", g), 3 * (CYCLES - 1) * (n + 1) - 2 + k)
                    else:
                        dve.wait_ge(s("upd_pool", g), (CYCLES - 1) * (n + 1))
                    add_half(st[:, 4 * g + k], 4 * g + k).then_inc(s("half_added", g), 1)

            def finish(n, g, k):
                if k < 3:
                    dve.wait_ge(s("mul_done", g), 3 * (CYCLES * (n + 1) - 1) + k + 1)
                else:
                    dve.wait_ge(s("mul_pool", g), CYCLES * (n + 1))
                dve.wait_ge(s("half_added", g), 4 * n + k + 1)
                add_half(tmp[:, g, k], 4 * g + k).then_inc(s("x_new"), 1)

            def cycles(n):
                for c in range(CYCLES - 1):
                    for g in range(G):
                        if c == 0:
                            dve.wait_ge(s("gth_done", g), n + 1)
                            nc.vector.tensor_scalar(s0[:, 4 * g:4 * g + 4], gth[:, 4 * g:4 * g + 4], ar_gf[:],
                                                    BASE_COUPLING, ALU.mult, ALU.add).then_inc(s("s0_ready", g), 1)
                            dve.wait_ge(s("s0_ready", g), n + 1)
                        update(CYCLES * n + c, g)
                        if c == CYCLES - 2:
                            add_state(n, g)

            def row_max(i, u, c):
                dve.wait_ge(s("s_ready"), 2 * ((i + 1) * H + u) + c + 1)
                half, hl = u // HALF, u % HALF
                nc.vector.tensor_reduce(nmax[:, half, 2 * c:2 * c + 2, hl % 2, hl // 2:hl // 2 + 1],
                                        ps[:, 2 + 2 * c:4 + 2 * c, :], AX_X, ALU.max, negate=True)\
                    .then_inc(s("s_used"), 1)

            def split_max(b, half):
                n = 2 * b + half
                dve.wait_ge(s("s_used"), 2 * (b * H + (half + 1) * HALF))
                waits_for(dve, s("maxT_ready"), n)
                m = nmax[:, half]
                nc.vector.tensor_copy(nparts[:, :, :, 0], m).then_inc(s("n1"), 1)
                dve.wait_ge(s("n1"), n + 1)
                nc.vector.tensor_tensor(nres[:], m, nparts[:, :, :, 0], ALU.subtract).then_inc(s("nr1"), 1)
                dve.wait_ge(s("nr1"), n + 1)
                nc.vector.tensor_copy(nparts[:, :, :, 1], nres[:]).then_inc(s("n2"), 1)
                dve.wait_ge(s("n2"), n + 1)
                nc.vector.tensor_tensor(nparts[:, :, :, 2], nres[:], nparts[:, :, :, 1], ALU.subtract)\
                    .then_inc(s("n3"), 1)

            def normalise(i, lt):
                n = (i - 1) * T + lt
                dve.wait_ge(s("oT_ready"), n + 1)
                o = ps[:, 7, :].rearrange("p (h c) -> p h c", c=VC)
                nc.vector.reciprocal(rden[:, lt, :], o[:, :, DH]).then_inc(s("oT_rden"), 1)
                dve.wait_ge(s("oT_rden"), n + 1)
                waits_for(dve, s("onT_ready"), i - 1)
                nc.vector.tensor_tensor(on[:, lt].rearrange("p (h d) -> p h d", d=DH), o[:, :, 0:DH],
                                        rden[:, lt].unsqueeze(2).to_broadcast([P, H, DH]), ALU.mult)\
                    .then_inc(s("oT_used"), 1)

            def residual(i):
                dve.wait_ge(s("proj_ready"), i)
                nc.vector.tensor_tensor(batch_of(xs, i - 1), ps[:, 7, :], batch_of(xs, i - 1), ALU.add)\
                    .then_inc(s("proj_done"), 1)

            def batch_of(v, b):
                if isinstance(b, int):
                    return v[:, b].rearrange("p t d -> p (t d)")
                return v[:].rearrange("p b t d -> p (b t d)")[:, bass.ds(b * (T * D), T * D)]

            def swap(b, k):
                nc.vector.stream_shuffle(qksw[:, k], qkf[:, k], SWAPPED).then_inc(s("swapped"), 1)

            def iteration(i, q, first, last):
                a_on = first >= 0 and last <= B - 3
                s_on = first >= -1 and last <= B - 2
                b = i + 2
                tokens = batch_of(xs, b).rearrange("p (t d) -> p t d", t=T) if a_on else None
                for u in range(H):
                    if a_on and u == 0:
                        token_stats(LN_CALLS + b, [tokens], slice(q, q + 1))
                    if a_on and u == 1:
                        dve.wait_ge(s("ln_stats"), LN_CALLS + b + 1)
                    if s_on:
                        row_max(i, u, 0)
                    if a_on and u == 1:
                        token_variance(LN_CALLS + b, slice(q, q + 1))
                    if a_on and u == 2:
                        dve.wait_ge(s("ln_rstd"), LN_CALLS + b + 1)
                        waits_for(dve, s("xT_ready"), b - 1)
                        normalise_tokens(tokens, xn[:, q], q, s("xn_ready"))
                    if first >= 1 and 8 <= u < 8 + T:
                        normalise(i, u - 8)
                    if a_on and u in (4, 5):
                        dve.wait_ge(s("qk"[u - 4] + "_done"), b + 1)
                    if s_on:
                        row_max(i, u, 1)
                    if a_on and u in (4, 5):
                        swap(b, u - 4)
                    if u == 3 and first >= 0 and last <= B - 1:
                        split_max(i, 1)
                    if u == HALF + 1 and s_on:
                        split_max(i + 1, 0)
                    if first >= 1 and u == 14:
                        residual(i)

            def first_norm(b):
                dve.wait_ge(s("x_new"), b + 1)
                token_stats(LN_CALLS + b, [xs[:, b]], slice(b, b + 1))
                dve.wait_ge(s("ln_stats"), LN_CALLS + b + 1)
                token_variance(LN_CALLS + b, slice(b, b + 1))

            def first_normalise(b):
                dve.wait_ge(s("ln_rstd"), LN_CALLS + b + 1)
                normalise_tokens(xs[:, b], xn[:, b], b, s("xn_ready"))

            def rope_and_split_first_q():
                fa, fb, fc, fd = (xT[:, 0, j] for j in range(4))
                dve.wait_ge(s("cst_in"), 32)
                dve.wait_ge(s("q_done"), 1)
                swap(0, 0)
                nc.vector.tensor_tensor(fa, qkf[:, 0], cosb[:], ALU.mult).then_inc(s("first_q"), 1)
                dve.wait_ge(s("k_done"), 1)
                swap(0, 1)
                dve.wait_ge(s("swapped"), 1)
                nc.vector.tensor_tensor(fb, qksw[:, 0], sinb[:], ALU.mult).then_inc(s("first_q"), 1)
                dve.wait_ge(s("first_q"), 2)
                nc.vector.tensor_tensor(fc, fa, fb, ALU.add).then_inc(s("first_q"), 1)
                nc.vector.tensor_tensor(parts[:, 0, 0], fa, fb, ALU.add).then_inc(s("first_q"), 1)
                dve.wait_ge(s("first_q"), 4)
                nc.vector.tensor_tensor(fd, fc, parts[:, 0, 0], ALU.subtract).then_inc(s("first_q"), 1)
                nc.vector.tensor_tensor(parts[:, 0, 1], fc, parts[:, 0, 0], ALU.subtract).then_inc(s("first_q"), 1)
                dve.wait_ge(s("first_q"), 6)
                nc.vector.tensor_tensor(parts[:, 0, 2], fd, parts[:, 0, 1], ALU.subtract).then_inc(s("first_q"), 1)

            for pair in range(LN_CALLS // 2):
                pair_variance(0, pair)
            for pair in range(LN_CALLS // 2):
                pair_normalise(0, pair)
            halves()
            for pair in range(LN_CALLS // 2, LN_CALLS):
                pair_variance(0, pair)
            for pair in range(LN_CALLS // 2, LN_CALLS):
                pair_normalise(0, pair)
            nc.vector.tensor_copy(ident_bf[:], ident[:]).then_inc(s("ident_ready"), 1)
            dve.wait_ge(s("halves"), 1)
            cycles(0)
            couple(CYCLES - 1, 0)
            multiply(0, 0)
            finish(0, 0, 0)
            multiply(0, 1)
            first_norm(0)
            finish(0, 0, 1)
            multiply(0, 2)
            first_normalise(0)
            finish(0, 0, 2)
            finish(0, 0, 3)
            rope_and_split_first_q()
            first_norm(1)
            first_normalise(1)
            couple(CYCLES - 1, 1)
            for k in range(3):
                multiply(1, k)
            for k in range(4):
                finish(0, 1, k)
            for k in range(2):
                dve.wait_ge(s("qk"[k] + "_done"), 2)
                swap(1, k)
            dve.wait_ge(s("x_new"), B)
            pipeline(dve, iteration)
            dve.wait_ge(s("proj_done"), B - 2)
            for pair in range(LN_CALLS - 1):
                pair_variance(1, pair)
            for pair in range(LN_CALLS // 2):
                pair_normalise(1, pair)
            iteration(B - 1, 1, B - 1, B - 1)
            iteration(B, 0, B, B)
            pair_normalise(1, LN_CALLS - 2)
            dve.wait_ge(s("proj_done"), B)
            pair_variance(1, LN_CALLS - 1)
            pair_normalise(1, LN_CALLS - 1)
            cycles(1)
            for g in range(G):
                couple(2 * CYCLES - 1, g)
                for k in range(3):
                    multiply(g, k)
                for k in range(4):
                    finish(1, g, k)

        @block.scalar
        def _(act):
            def evacuate(dst, src):
                return nc.scalar.activation(dst, src, ACT.Copy)

            def turned(it, g, first=False):
                for k in range(4):
                    act.wait_ge(s("T_ready", g), 4 * it + k + 1)
                    nc.scalar.activation(xT[:, g, k], ps[:, 4 * g + k, :], ACT.Copy,
                                         accum_out=gm[:, 4 * g + k:4 * g + k + 1] if first else None)\
                        .then_inc(s("T_copied", g), 1)

            def gelu1(it, g, ks):
                for k in ks:
                    act.wait_ge(s("L1_ready", g), 4 * it + k + 1)
                    nc.scalar.activation(h1[:, g, k], ps[:, 4 * g + k, :], ACT.Gelu, bias=b1s[:])\
                        .then_inc(s("h1_done", g), 1)

            def gelu2(it, g, ks=(0, 1)):
                for k in ks:
                    act.wait_ge(s("L2_ready", g), 2 * it + k + 1)
                    nc.scalar.activation(h2[:, g, k], ps[:, 4 * g + k, :], ACT.Gelu, bias=b2s[:])\
                        .then_inc(s("h2_done", g), 1)

            def gelu3(it, g):
                act.wait_ge(s("L3_ready", g), it + 1)
                nc.scalar.activation(h3[:, g], ps[:, 4 * g + 2, :], ACT.Gelu, bias=b3s[:]).then_inc(s("h3_done", g), 1)

            def tanh(it, g):
                act.wait_ge(s("L4_ready", g), it + 1)
                nc.scalar.activation(th[:, g].rearrange("p b t -> p t b"),
                                     ps[:, 4 * g + 3, 0:4 * T].rearrange("p (t b) -> p t b", b=4),
                                     ACT.Tanh, bias=b4h[:], scale=0.5).then_inc(s("th_done", g), 1)

            def global1(n, g):
                act.wait_ge(s("gh1_ready", g), n + 1)
                nc.scalar.activation(gh1[:, 4 * g:4 * g + 4], global_out(g, 0)[0:64], ACT.Gelu, bias=gb1s[:],
                                     scale=1.0 / S).then_inc(s("gh1_done", g), 1)

            def global2(n, g):
                act.wait_ge(s("gh2_ready", g), n + 1)
                nc.scalar.activation(gh2[:, 4 * g:4 * g + 4], global_out(g, 1)[0:32], ACT.Gelu, bias=gb2s[:])\
                    .then_inc(s("gh2_done", g), 1)

            def global3(n, g):
                act.wait_ge(s("gth_ready", g), n + 1)
                nc.scalar.activation(gth[:, 4 * g:4 * g + 4], global_out(g, 2), ACT.Tanh, bias=gb3h[:], scale=0.5)\
                    .then_inc(s("gth_done", g), 1)

            def first_cycle(n):
                it = CYCLES * n
                turned(it, 0, True)
                if n == 0:
                    act.wait_ge(s("w1_in"), 32)
                gelu1(it, 0, range(4))
                if n == 0:
                    act.wait_ge(s("wc_in"), 16 * WC_DMAS)
                gelu2(it, 0, (0,))
                if n == 1:
                    take_onT(B)
                gelu2(it, 0, (1,))
                global1(n, 0)
                gelu3(it, 0)
                global2(n, 0)
                act.wait_ge(s("halves"), 1)
                tanh(it, 0)
                global3(n, 0)
                turned(it, 1, True)
                gelu1(it, 1, (0, 1))
                global1(n, 1)
                gelu1(it, 1, (2, 3))
                global2(n, 1)
                gelu2(it, 1)
                global3(n, 1)

            def feed_forward(n):
                first_cycle(n)
                with act.Fori(1, CYCLES) as c:
                    it = CYCLES * n + c
                    for g in range(G):
                        turned(it, g)
                        gelu3(it - (g == 0), 1 - g)
                        tanh(it - (g == 0), 1 - g)
                        gelu1(it, g, range(4))
                        gelu2(it, g)
                gelu3(CYCLES * n + CYCLES - 1, 1)
                tanh(CYCLES * n + CYCLES - 1, 1)

            def exps(i, u):
                for mt in range(T):
                    act.wait_ge(s("st_ready"), (i * H + u) * T + mt + 1)
                    if mt == 0 and u % 4 == 0:
                        waits_for(act, s("pv_ready"), 4 * i + u // 4 - 1)
                    nc.scalar.activation(probs[:, u % 8, S * mt:S * (mt + 1)], ps[:, mt % 2, :],
                                         ACT.Exp, scale=SCALE).then_inc(s("exp_done"), 1)

            def take_pv(i, q, u):
                g = (u - 8) // 4
                b = i if g >= 0 else i - 1
                g = g % 4
                act.wait_ge(s("pv_ready"), 4 * b + g + 1)
                waits_for(act, s("oT_ready"), T * (b - (g == 0)))
                evacuate(output_T(g, (q if b is i else 1 - q)), ps[:, 6, :]).then_inc(s("pv_used"), 1)

            def iteration(i, q, first, last):
                for u in range(H):
                    if first >= 0 and last <= B - 1:
                        exps(i, u)
                    if first >= 0 and last <= B - 3:
                        b = i + 2
                        if u == 2:
                            act.wait_ge(s("xT_ready"), b + 1)
                            evacuate(xnT[:, q], ps[:, 7, :]).then_inc(s("xnT_done"), 1)
                        if u in (3, 4):
                            k = u - 3
                            act.wait_ge(s("qk"[k] + "_ready"), b + 1)
                            waits_for(act, s("rope_b"), 2 * b - 2 + k)
                            evacuate(qkf[:, k], ps[:, 7, :]).then_inc(s("qk"[k] + "_done"), 1)
                    if u == 5 and first >= 0 and last <= B - 1:
                        take_max(i, 1)
                    if u == 11 and first >= -1 and last <= B - 2:
                        take_max(i + 1, 0)
                    if u == 6 and first >= -1 and last <= B - 2:
                        act.wait_ge(s("v_ready"), i + 2)
                        evacuate(vst[:, 1 - q, :, :, 0:DH].rearrange("p t h d -> p (t h) d"),
                                 ps[:, 7, :].rearrange("p (a d) -> p a d", d=DH)).then_inc(s("v_done"), 1)
                    if u == 12 and first >= 1:
                        take_onT(i)
                    if u % 4 == 3:
                        if (u > 3 and first >= 0 and last <= B - 1) or (u == 3 and first >= 1):
                            take_pv(i, q, u + 1)

            def take_onT(i):
                act.wait_ge(s("onT_ready"), i)
                waits_for(act, s("proj_ready"), i - 1)
                evacuate(onT[:], ps[:, 7, :]).then_inc(s("onT_done"), 1)

            def take_max(b, half):
                n = 2 * b + half
                act.wait_ge(s("maxT_ready"), n + 1)
                waits_for(act, s(f"mrow_out{1 - half}"), 16 * (b + half))
                evacuate(mrow[:], ps[0:6 * PAIRS, 7, 0:S // 2].bitcast(BF16)).then_inc(s("maxT_done"), 1)

            feed_forward(0)
            act.wait_ge(s("wT_ready"), 1)
            evacuate(wT[:].rearrange("p a c -> p (a c)"), ps[:, 1, :]).then_inc(s("wT_copied"), 1)
            for b in range(2):
                act.wait_ge(s("xT_ready"), b + 1)
                evacuate(xnT[:, b], ps[:, 0, :]).then_inc(s("xnT_done"), 1)
                for k in range(2):
                    act.wait_ge(s("qk"[k] + "_ready"), b + 1)
                    if b == 1 and k == 0:
                        act.wait_ge(s("first_q"), 2)
                    if b == 1 and k == 1:
                        act.wait_ge(s("rope_b"), 1)
                    evacuate(qkf[:, k], ps[:, 1 - k, :]).then_inc(s("qk"[k] + "_done"), 1)
            pipeline(act, iteration)
            iteration(B - 1, 1, B - 1, B - 1)
            take_pv(B, 0, 4)
            feed_forward(1)

        @block.tensor
        def _(pe):
            def turn(it, n, g, k, first):
                if first:
                    pe.wait_ge(s("ln_out"), B * n + 4 * g + k + 1)
                elif k < 3:
                    pe.wait_ge(s("upd_dve", g), 3 * (it - n) - 2 + k)
                else:
                    pe.wait_ge(s("upd_pool", g), it - n)
                for t in range(T):
                    last = nc.tensor.transpose(ps[:, 4 * g + k, P * t:P * t + P], st[:, 4 * g + k, t], ident[:])
                last.then_inc(s("T_ready", g), 1)

            def layer1(it, g, ks):
                for k in ks:
                    pe.wait_ge(s("T_copied", g), 4 * it + k + 1)
                    nc.tensor.matmul(ps[:, 4 * g + k, :], w1s[:], xT[:, g, k], start=True, stop=True)\
                        .then_inc(s("L1_ready", g), 1)

            def layer2(it, g, pairs=(0, 1)):
                for pr in pairs:
                    pe.wait_ge(s("h1_done", g), 4 * it + 2 * pr + 2)
                    for k in range(2):
                        last = nc.tensor.matmul(ps[64 * k:64 * k + 64, 4 * g + pr, :], w2s[:], h1[:, g, 2 * pr + k],
                                                start=True, stop=True)
                    last.then_inc(s("L2_ready", g), 1)

            def layer3(it, g):
                pe.wait_ge(s("h2_done", g), 2 * it + 2)
                for pr in range(2):
                    last = nc.tensor.matmul(ps[64 * pr:64 * pr + 64, 4 * g + 2, :], w3s[:], h2[:, g, pr],
                                            start=True, stop=True)
                last.then_inc(s("L3_ready", g), 1)

            def layer4(it, g):
                pe.wait_ge(s("h3_done", g), it + 1)
                for t in range(T):
                    last = nc.tensor.matmul(ps[:, 4 * g + 3, 4 * t:4 * t + 4], h3[:, g, P * t:P * t + P], w4s[:],
                                            start=True, stop=True)
                last.then_inc(s("L4_ready", g), 1)

            def global1(n, g):
                pe.wait_ge(s("T_copied", g), 4 * CYCLES * n + 4)
                if g == 0:
                    pe.wait_ge(s("h2_done", 0), 2 * CYCLES * n + 1)
                nc.tensor.matmul(global_out(g, 0)[0:64], g1s[:], gm[:, 4 * g:4 * g + 4], start=True, stop=True)\
                    .then_inc(s("gh1_ready", g), 1)

            def global2(n, g):
                pe.wait_ge(s("gh1_done", g), n + 1)
                if g == 1:
                    pe.wait_ge(s("gth_done", 0), n + 1)
                nc.tensor.matmul(global_out(g, 1)[0:32], g2s[:], gh1[:, 4 * g:4 * g + 4], start=True, stop=True)\
                    .then_inc(s("gh2_ready", g), 1)

            def global3(n, g):
                pe.wait_ge(s("gh2_done", g), n + 1)
                nc.tensor.matmul(global_out(g, 2), g3r[:], gh2[:, 4 * g:4 * g + 4], start=True, stop=True)\
                    .then_inc(s("gth_ready", g), 1)

            def first_cycle(n):
                it = CYCLES * n

                def between(u):
                    if n == 1:
                        side_work(B, 0, u, B, B)

                for k in range(4):
                    turn(it, n, 0, k, True)
                if n == 0:
                    pe.wait_ge(s("w1_in"), 32)
                for k in range(4):
                    layer1(it, 0, (k,))
                    between(7 + k)
                if n == 0:
                    pe.wait_ge(s("wc_in"), 16 * WC_DMAS)
                layer2(it, 0, (0,))
                between(12)
                layer2(it, 0, (1,))
                between(13)
                global1(n, 0)
                layer3(it, 0)
                global2(n, 0)
                layer4(it, 0)
                pe.wait_ge(s("halves"), 1)
                global3(n, 0)
                for k in range(4):
                    turn(it, n, 1, k, True)
                layer1(it, 1, (0, 1))
                global1(n, 1)
                layer1(it, 1, (2, 3))
                global2(n, 1)
                layer2(it, 1)
                global3(n, 1)

            def feed_forward(n):
                first_cycle(n)
                with pe.Fori(1, CYCLES) as c:
                    it = CYCLES * n + c
                    for g in range(G):
                        for k in range(4):
                            if g == 0 and k == 1:
                                pe.wait_ge(s("gth_done", 1), n + 1)
                            turn(it, n, g, k, False)
                        layer3(it - (g == 0), 1 - g)
                        layer1(it, g, (0,))
                        layer4(it - (g == 0), 1 - g)
                        layer1(it, g, (1, 2, 3))
                        layer2(it, g)
                layer3(CYCLES * n + CYCLES - 1, 1)
                layer4(CYCLES * n + CYCLES - 1, 1)

            def scores_T(i, q, u, mt):
                n = (i * H + u) * T + mt
                if u % HALF == 0 and mt == 0:
                    pe.wait_ge(s(f"mrow_out{u // HALF}"), 16 * i + 16)
                waits_for(pe, s("exp_done"), n - 1)
                nc.tensor.matmul(ps[:, mt % 2, :], kst[:, q, u // 2, u % 2, P * mt:P * mt + P],
                                 qst[:, q, u // 2, :], start=True, stop=True).then_inc(s("st_ready"), 1)

            def scores(i, q, u, lt):
                if u % HALF == 0 and lt == 0:
                    pe.wait_ge(s(f"fill{u // HALF}"), FILL * (i + 2))
                if lt % 2 == 0:
                    waits_for(pe, s("s_used"), 2 * ((i + 1) * H + u) + lt // 2 - 1)
                mm = nc.tensor.matmul(ps[:, 2 + lt, :], qst[0:MAX_ROW, 1 - q, u // 2, P * lt:P * lt + P],
                                      kst[0:MAX_ROW, 1 - q, u // 2, u % 2, :], start=True, stop=True)
                if lt % 2 == 1:
                    mm.then_inc(s("s_ready"), 1)

            def products(i, q, u):
                g = u // 4 - 1
                b, qb = (i, q) if g >= 0 else (i - 1, 1 - q)
                g, mt = g % 4, u % 4
                if mt == 0:
                    pe.wait_ge(s("exp_done"), (4 * b + g + 1) * 4 * T)
                    waits_for(pe, s("pv_used"), 4 * b + g)
                    if g == 0:
                        pe.wait_ge(s("v_done"), b + 1)
                for j in range(4):
                    h = 4 * g + j
                    last = nc.tensor.matmul(ps[32 * j:32 * j + 32, 6, :], vst[:, qb, mt, h, :],
                                            probs[:, h % 8, S * mt:S * mt + S], start=(mt == 0), stop=(mt == T - 1))
                if mt == T - 1:
                    last.then_inc(s("pv_ready"), 1)

            def project(b, w, ready, xq):
                nc.tensor.matmul(ps[:, 7, :], wT[:, w], xnT[:, xq], start=True, stop=True).then_inc(s(ready), 1)

            def turn_max(b, half):
                pe.wait_ge(s("n3"), 2 * b + half + 1)
                for t in range(T):
                    last = nc.tensor.transpose(ps[0:6 * PAIRS, 7, 0:S // 2].bitcast(BF16)[:, P * t:P * t + P],
                                               nparts[:, t].rearrange("p a k h -> p (a k h)"), ident_bf[:])
                last.then_inc(s("maxT_ready"), 1)

            def side_work(i, q, u, first, last_i):
                a_on = first >= 0 and last_i <= B - 3
                c_on = first >= 1
                if u == 2 and a_on:
                    b = i + 2
                    waits_for(pe, s("proj_done"), i - 1)
                    waits_for(pe, s("maxT_done"), 2 * (i + 1) - 1)
                    waits_for(pe, s("v_done"), i + 1)
                    waits_for(pe, s("k_done"), i + 2)
                    pe.wait_ge(s("xn_ready"), b + 1)
                    for t in range(T):
                        last = nc.tensor.transpose(ps[:, 7, P * t:P * t + P], xn[:, q, t], ident[:])
                    last.then_inc(s("xT_ready"), 1)
                if u == 3 and a_on:
                    pe.wait_ge(s("xnT_done"), i + 3)
                    project(i + 2, 0, "q_ready", q)
                if u == 4 and a_on:
                    pe.wait_ge(s("q_done"), i + 3)
                    project(i + 2, 1, "k_ready", q)
                if u == 5 and first >= 0 and last_i <= B - 1:
                    waits_for(pe, s("k_done"), i + 3 if a_on else 0)
                    waits_for(pe, s("proj_done"), i - 1 if not a_on else 0)
                    turn_max(i, 1)
                if u == 6 and first >= -1 and last_i <= B - 2:
                    waits_for(pe, s("k_done"), i + 3 if a_on else 0)
                    waits_for(pe, s("maxT_done"), 2 * i + 2 if first >= 0 else 0)
                    for t in range(T):
                        last = nc.tensor.matmul(ps[:, 7, P * t:P * t + P], xnT[:, 1 - q, P * t:P * t + P], wT[:, 2],
                                                start=True, stop=True)
                    last.then_inc(s("v_ready"), 1)
                if c_on and 7 <= u < 7 + T:
                    lt = u - 7
                    if lt == 0:
                        pe.wait_ge(s("pv_used"), 4 * i)
                        waits_for(pe, s("proj_done"), i - 1)
                        waits_for(pe, s("v_done"), i + 2 if last_i <= B - 2 else 0)
                        waits_for(pe, s("maxT_done"), 2 * i + 2 if last_i <= B - 1 else 0)
                    waits_for(pe, s("oT_used"), T * (i - 1) + lt)
                    for g in range(4):
                        last = nc.tensor.transpose(ps[:, 7, P * g:P * g + P], output_T(g, 1 - q)[:, P * lt:P * lt + P], ident[:])
                    last.then_inc(s("oT_ready"), 1)
                if u == 11 and first >= -1 and last_i <= B - 2:
                    waits_for(pe, s("oT_used"), T * i if c_on else 0)
                    pe.wait_ge(s("v_done"), i + 2)
                    turn_max(i + 1, 0)
                if c_on and u == 12:
                    pe.wait_ge(s("oT_used"), T * i)
                    waits_for(pe, s("maxT_done"), 2 * i + 3 if last_i <= B - 2 else 0)
                    for t in range(T):
                        last = nc.tensor.transpose(ps[:, 7, P * t:P * t + P], on[:, t], ident[:])
                    last.then_inc(s("onT_ready"), 1)
                if c_on and u == 13:
                    pe.wait_ge(s("onT_done"), i)
                    for t in range(T):
                        last = nc.tensor.matmul(ps[:, 7, P * t:P * t + P], onT[:, P * t:P * t + P], wT[:, 3],
                                                start=True, stop=True)
                    last.then_inc(s("proj_ready"), 1)

            def iteration(i, q, first, last):
                for u in range(H):
                    st_on = first >= 0 and last <= B - 1
                    s_on = first >= -1 and last <= B - 2
                    pv_on = (u >= 4 and st_on) or (u < 4 and first >= 1)
                    for t in (0, 1):
                        if st_on:
                            scores_T(i, q, u, t)
                        if s_on:
                            scores(i, q, u, t)
                    if pv_on:
                        products(i, q, u)
                    for t in (2, 3):
                        if st_on:
                            scores_T(i, q, u, t)
                        if s_on:
                            scores(i, q, u, t)
                    side_work(i, q, u, first, last)

            pe.wait_ge(s("ident_in"), 16)
            feed_forward(0)
            pe.wait_ge(s("w_in"), 16 * 10)
            for j in range(4):
                last = nc.tensor.transpose(ps[:, 1, P * j:P * j + P], wnat[:, j], ident[:])
            last.then_inc(s("wT_ready"), 1)
            for b in range(2):
                pe.wait_ge(s("xn_ready"), b + 1)
                waits_for(pe, s("k_done"), b)
                for t in range(T):
                    last = nc.tensor.transpose(ps[:, 0, P * t:P * t + P], xn[:, b, t], ident[:])
                last.then_inc(s("xT_ready"), 1)
                pe.wait_ge(s("xnT_done"), b + 1)
                if b == 0:
                    pe.wait_ge(s("wT_copied"), 1)
                waits_for(pe, s("q_done"), b)
                for k in range(2):
                    nc.tensor.matmul(ps[:, 1 - k, :], wT[:, k], xnT[:, b], start=True, stop=True)\
                        .then_inc(s("qk"[k] + "_ready"), 1)
            pe.wait_ge(s("th_done", 1), CYCLES)
            pe.wait_ge(s("ident_ready"), 1)
            pe.wait_ge(s("setup_dve"), 3)
            pe.wait_ge(s("ones_dma"), 16 * 4)
            pipeline(pe, iteration)
            iteration(B - 1, 1, B - 1, B - 1)
            for u in range(T):
                products(B, 0, u)
            feed_forward(1)


_INS = ['L0_attn_x', 'L0_attn_w_qkv', 'L0_attn_w_out',
        'L0_ffn_cn_w1', 'L0_ffn_cn_b1', 'L0_ffn_cn_w2', 'L0_ffn_cn_b2',
        'L0_ffn_cn_w3', 'L0_ffn_cn_b3', 'L0_ffn_cn_w4', 'L0_ffn_cn_b4',
        'L0_ffn_gc_w1', 'L0_ffn_gc_b1', 'L0_ffn_gc_w2', 'L0_ffn_gc_b2', 'L0_ffn_gc_w3', 'L0_ffn_gc_b3',
        'L0_ffn_adaptive_range']


def shape_constants(S, D, H):
    import numpy as np
    dh = D // H
    half = dh // 2
    inv_freq = (np.float32(1.0) / np.float32(10000.0) ** (np.arange(half, dtype=np.float32) / np.float32(half)))
    ang = np.arange(S, dtype=np.float32)[:, None] * inv_freq.astype(np.float32)[None, :]
    cos, sin = np.cos(ang).astype(np.float32).T, np.sin(ang).astype(np.float32).T
    cos = np.tile(np.repeat(np.concatenate([cos, cos]), H // 4, axis=0), (4, 1))
    sin = np.tile(np.repeat(np.concatenate([-sin, sin]), H // 4, axis=0), (4, 1))
    return (np.ascontiguousarray(cos), np.ascontiguousarray(sin), np.eye(128, dtype=np.float32))


def kernel(**inputs):
    import numpy as _np
    import concourse.bacc as _bacc
    from concourse import mybir as _mybir
    from concourse.bass_utils import run_bass_kernel_spmd as _run

    nc = _bacc.Bacc("TRN2", target_bir_lowering=False, num_devices=1)
    arrays, args = {}, []

    def give(name, a):
        arrays[name] = a
        return nc.dram_tensor(name, a.shape, _mybir.dt.from_np(a.dtype), kind="ExternalInput").ap()

    for name in _INS:
        args.append(give(f"in_{name}_dram", _np.ascontiguousarray(inputs[name])))
    B, S, D = inputs['L0_attn_x'].shape
    tables = [give(f"in_{n}_dram", a) for n, a in zip(("cos", "sin", "ident"), shape_constants(S, D, 16))]
    out = nc.dram_tensor("out_0_dram", (B, S, D), _mybir.dt.float32, kind="ExternalOutput").ap()
    macaron_kernel(nc, args[0], args[1], args[2], args[3:11], args[11:17], args[17], *tables, out)
    r = _run(nc, [arrays], core_ids=[0])
    return r.results[0]["out_0_dram"]
```

```python
from contextlib import ExitStack

import concourse.bass as bass
from concourse import mybir

P = 128
F32 = mybir.dt.float32
BF16 = mybir.dt.bfloat16
ALU = mybir.AluOpType
ACT = mybir.ActivationFunctionType
AX_X = mybir.AxisListType.X

EPS = 1e-5
BASE_COUPLING = 0.1
GF_SHARE, TF_SHARE = 0.7, 0.3
CYCLES = 3

Q_PARTS = [0, 0, 0, 1, 1, 2]
K_PARTS = [0, 1, 2, 0, 1, 0]
TERMS = len(Q_PARTS)


def macaron_kernel(nc, x, w_qkv, w_out, cn, gc, adaptive_range, cos_t, sin_t, ident_t, out):
    B, S, D = x.shape
    H, DH = 16, D // 16
    T = S // P
    HP = H // 2
    HALF = H // 2
    PAIRS = HALF // 2
    G = B // 4
    HEAD_ROWS = TERMS * DH
    MAX_ROW = 2 * HEAD_ROWS
    ROWS = MAX_ROW + 6
    SCALE = float(DH) ** -0.5
    VC = 32
    (w1, b1, w2, b2, w3, b3, w4, b4), (g1, gb1, g2, gb2, g3, gb3) = cn, gc

    with ExitStack() as ctx:
        def sb(name, shape, dt=F32):
            return ctx.enter_context(nc.sbuf_tensor(name, shape, dt))

        def sem(name):
            return ctx.enter_context(nc.semaphore(name))

        ps = ctx.enter_context(nc.psum_tensor("ps", [P, 8, 512], F32))

        xs = sb("xs", [P, B, T, D])
        st = sb("st", [P, B, T, D])
        ident = sb("ident", [P, P])
        ident_bf = sb("ident_bf", [P, P], BF16)
        cosb, sinb = sb("cosb", [P, S]), sb("sinb", [P, S])
        w1s, w2s, w3s = sb("w1s", [P, 128]), sb("w2s", [P, 64]), sb("w3s", [P, 64])
        w4s = sb("w4s", [P, 4])
        g1s, g2s, g3s, g3r = sb("g1s", [P, 64]), sb("g2s", [64, 32]), sb("g3s", [32, 1]), sb("g3r", [32, P])
        b1s, b2s, b3s, b4s = sb("b1s", [P, 1]), sb("b2s", [P, 1]), sb("b3s", [P, 1]), sb("b4s", [P, 1])
        gb1s, gb2s, gb3s = sb("gb1s", [64, 1]), sb("gb2s", [32, 1]), sb("gb3s", [P, 1])
        b4h, gb3h = sb("b4h", [P, 1]), sb("gb3h", [P, 1])
        ar, ar_tf, ar_gf = sb("ar", [P, 1]), sb("ar_tf", [P, 1]), sb("ar_gf", [P, 1])
        wT = sb("wT", [P, 4, D])
        stats, mv = sb("stats", [P, B, T, 6]), sb("mv", [P, B, T, 2])
        var, rstd, minus_half = sb("var", [P, B, T]), sb("rstd", [P, B, T]), sb("minus_half", [P, B, T])
        gm, gh1, gh2, gth = sb("gm", [P, B]), sb("gh1", [64, B]), sb("gh2", [32, B]), sb("gth", [P, B])
        s0 = sb("s0", [P, B])
        th = sb("th", [P, G, 4, T])
        cs = sb("cs", [P, G, 3, 4 * T])
        big = sb("big", [P, 8, T * S])
        by_group = big[:].rearrange("p (g j) (b s) -> p g j b s", g=G, b=4)
        xT, h1 = by_group[:, :, 0], by_group[:, :, 1]
        tmp = big[:].rearrange("p (g j) (b t d) -> p g j b t d", g=G, b=4, t=T)[:, :, 2]
        h2, h3 = by_group[:, :, 3, 0:2], by_group[:, :, 3, 2]
        wnat = big[:, 7, 3 * S:3 * S + 4 * D].rearrange("p (a d) -> p a d", a=4)
        probs = big
        xn = st[:, 0:2]
        ra, rb = st[:, 2].rearrange("p t d -> p (t d)"), st[:, 3].rearrange("p t d -> p (t d)")
        oT = st[:, 4:8].rearrange("p g t d -> p g (t d)")
        oT0 = sb("oT0", [P, S])
        on_both = sb("on_both", [P, 2 * S])
        on, onT = on_both[:, 0:S].rearrange("p (t d) -> p t d", t=T), on_both[:, S:2 * S]
        first_q_parts = big[:, 1, 0:3 * S // 2].bitcast(BF16).rearrange("p (a s) -> p a s", a=3)
        second_k_parts = on_both[:, 0:3 * S // 2].bitcast(BF16).rearrange("p (a s) -> p a s", a=3)
        xnT = sb("xnT", [P, 2, S])
        qkf, qksw = sb("qkf", [P, 2, S]), sb("qksw", [P, 2, S])
        rc, rd = sb("rc", [P, S]), sb("rd", [P, S])
        parts = sb("parts", [P, 2, 3, S], BF16)
        qst = sb("qst", [ROWS, 2, HP, S], BF16)
        kst = sb("kst", [ROWS, 2, HP, 2, S], BF16)
        orow = sb("orow", [3, S], BF16)
        vst = sb("vst", [P, 2, T, H, VC])
        nmax = sb("nmax", [P, 2, T, 2, PAIRS])
        nres = sb("nres", [P, T, 2, PAIRS])
        nparts = sb("nparts", [P, T, 2, 3, PAIRS], BF16)
        mrow = sb("mrow", [6 * PAIRS, S], BF16)
        rden = sb("rden", [P, T, H])

        S_ = {}
        for name in (
            "ident_in half_ready ln_var x_first x_in0 x_in1 x_in2 x_in3 w_in w1_in w2_in cst_in wc_in st_out setup_dve setup_pool vst_zero vst_one ones_dma ident_ready halves "
            "wT_ready wT_copied ln_stats ln_mv ln_rstd ln_out x_new first_q "
            "xn_ready xT_ready xnT_done q_ready q_done k_ready k_done v_ready v_done swapped rope_a rope_b "
            "rope_c part1 res1 part2 parts_ready fill_even0 fill_even1 fill0 fill1 st_ready st_used s_ready s_used "
            "exp_done pv_ready pv_used pv_step n1 nr1 n2 n3 maxT_ready maxT_done mrow_out0 mrow_out1 "
            "oT_ready oT_rden oT_used on_done onT_ready onT_done proj_ready proj_done kept0 kept1"
        ).split():
            S_[name] = sem(name)
        for g in range(G):
            for name in "T_ready T_copied L1_ready h1_done L2_ready h2_done L3_ready h3_done L4_ready th_done cs0 cs1 cs_ready mul_done upd_dve mul_pool upd_pool gh1_ready gh1_done gh2_ready gh2_done gth_ready gth_done s0_ready half_added".split():
                S_[name, g] = sem(f"{name}_{g}")

        def s(name, g=None):
            return S_[name] if g is None else S_[name, g]

        x_dram = x.rearrange("b (t p) d -> p b t d", p=P)
        out_dram = out.rearrange("b (t p) d -> p b t d", p=P)
        col = lambda v: v.rearrange("(p a) -> p a", a=1)

        def waits_for(eng, semaphore, count):
            if not isinstance(count, int) or count > 0:
                eng.wait_ge(semaphore, count)

        block = ctx.enter_context(nc.Block())
        WC_DMAS = 15
        SWAP_ROWS = PAIRS * DH // 2
        SWAPPED = [(r + SWAP_ROWS) % (2 * SWAP_ROWS) for r in range(2 * SWAP_ROWS)]
        LEAD = H - 4
        LAST_CALLS = B // 2
        FILL = 16 * 2 * 2 * TERMS

        def pipeline(eng, iteration):
            for i in (-1, 0, 1):
                iteration(i, i % 2, i, i)
            with eng.Fori(1, B // 2 - 1) as j:
                for q in range(2):
                    iteration(2 * j + q, q, 2, B - 3)
            iteration(B - 2, (B - 2) % 2, B - 2, B - 2)

        def ahead(i, q, u):
            b, q, h = (i, q, u + LEAD) if u < H - LEAD else (i + 1, 1 - q, u - (H - LEAD))
            n = b * H + h
            if even_first(b):
                h = h // HALF * HALF + 2 * h % HALF + h % HALF // PAIRS
            return b, q, n, h

        def even_first(b):
            return isinstance(b, int) and b == 0

        def parts_of(b, k):
            return second_k_parts if k == 1 and isinstance(b, int) and b == 1 else parts[:, k]

        def filled(batches):
            return FILL * batches - FILL // 2

        def maxima_on(first, last, u):
            return (first >= 0 and last <= B - 1) if u < H - LEAD else (first >= -1 and last <= B - 2)

        def output_T(g, q):
            return oT0[:] if g == 0 and q else oT[:, g]

        def last_heads(i, u):
            return isinstance(i, int) and i == B - 1 and u > H - LEAD

        OUTPUT_AT = {6: 0, 8: 1, 10: 2, 11: 3}

        def score_bank(i, u, mt):
            return mt if last_heads(i, u) else mt % 2

        def global_out(g, step):
            return ps[:, (g + step) % 2, 0:4]

        def wait_for_pv(eng, i, q, u):
            b, q, g = (i, q, u // 4 - 1) if u > 3 else (i - 1, 1 - q, 3)
            eng.wait_ge(s("pv_ready"), 4 * b + g + 1)
            waits_for(eng, s("oT_ready"), T * (b - (g == 0)))
            return output_T(g, q), ps[:, 6, :]

        def coupling(g, k, a):
            v = cs[:, g, a:a + 2, k]
            return v.rearrange("p u t -> p t u").unsqueeze(3).to_broadcast([P, k.stop - k.start, 2, 32])

        @block.sync
        def _(sp):
            def load_x(pair):
                sp.dma_start(xs[:, 2 * pair:2 * pair + 2], x_dram[:, 2 * pair:2 * pair + 2])\
                    .then_inc(s(f"x_in{pair}"), 16)

            sp.dma_start(xs[:, 0], x_dram[:, 0]).then_inc(s("x_first"), 16)
            sp.dma_start(xs[:, 1], x_dram[:, 1]).then_inc(s("x_in0"), 16)
            sp.dma_start(ident[:], ident_t).then_inc(s("ident_in"), 16)
            sp.dma_start(w1s[:], w1).then_inc(s("w1_in"), 16)
            sp.dma_start(b1s[:], col(b1)).then_inc(s("w1_in"), 16)
            load_x(1)
            sp.wait_ge(s("setup_dve"), 1)
            sp.dma_start(w2s[:], w2).then_inc(s("w2_in"), 16)
            sp.dma_start(b2s[:], b2.unsqueeze(0).to_broadcast([2, 64])).then_inc(s("w2_in"), 16)
            load_x(2)
            jobs = [(g1s[:], g1), (gb1s[:], col(gb1)), (b3s[:], b3.unsqueeze(0).to_broadcast([4, 32]))]
            jobs += [(w3s[64 * i:64 * i + 64, 32 * i:32 * i + 32], w3) for i in range(2)]
            jobs += [(w4s[32 * i:32 * i + 32, i:i + 1], w4) for i in range(4)]
            jobs += [(g2s[:], g2), (g3s[:], g3), (gb2s[:], col(gb2)),
                     (b4s[:], b4.partition_broadcast(P)), (gb3s[:], gb3.partition_broadcast(P)),
                     (ar[:], adaptive_range.partition_broadcast(P))]
            assert len(jobs) == WC_DMAS
            for dst, src in jobs:
                sp.dma_start(dst, src).then_inc(s("wc_in"), 16)
            load_x(3)
            sp.dma_start(wnat[:, 3], w_out).then_inc(s("w_in"), 16)
            for j in range(2):
                src = w_qkv[j * D:(j + 1) * D].rearrange("(f hp par d) c -> par f d hp c", f=2, par=2, d=DH)
                for par in range(2):
                    for f in range(2):
                        r = 64 * par + 32 * f
                        sp.dma_start(wnat[r:r + 32, j], src[par, f]).then_inc(s("w_in"), 16)
            sp.dma_start(wnat[:, 2], w_qkv[2 * D:3 * D]).then_inc(s("w_in"), 16)
            sp.dma_start(cosb[:], cos_t).then_inc(s("cst_in"), 16)
            sp.dma_start(sinb[:], sin_t).then_inc(s("cst_in"), 16)
            sp.wait_ge(s("setup_pool"), 1)
            for q in range(2):
                for par in range(2):
                    r = MAX_ROW + 3 * par
                    sp.dma_start(kst[r:r + 3, q, :, par, :], orow[:].unsqueeze(1).to_broadcast([3, HP, S]))\
                        .then_inc(s("ones_dma"), 16)

            def stack_part(q, half, k, part, source, pars=(0, 1), count=None):
                pairs = slice(PAIRS * half, PAIRS * (half + 1))
                for par in pars:
                    for t in range(TERMS):
                        if (Q_PARTS, K_PARTS)[k][t] == part:
                            r = HEAD_ROWS * par + t * DH
                            p0 = 64 * par + PAIRS * DH * half
                            dst = kst[r:r + DH, q, pairs, par, :] if k else qst[r:r + DH, q, pairs, :]
                            sp.dma_start(dst, source[p0:p0 + PAIRS * DH, part, :])\
                                .then_inc(count or s(f"fill{half}"), 16)

            def fill(b, q, half):
                if half == 0:
                    sp.wait_ge(s("parts_ready"), 2 * b + 1)
                if not isinstance(b, int) or b >= 2:
                    stack_free(b, half)
                if isinstance(b, int) and b == 1:
                    sp.wait_ge(s("s_ready"), 2 * (HALF * half + PAIRS) + 1)
                for k in range(2):
                    for part in range(3):
                        stack_part(q, half, k, part, parts_of(b, k))

            def stack_free(b, half):
                sp.wait_ge(s("st_ready"), T * (H * (b - 2) + HALF * (half + 1)))

            def iteration(i, q, first, last):
                if first >= 0 and last <= B - 2:
                    fill(i + 1, 1 - q, 1)
                if first >= 0 and last <= B - 3:
                    fill(i + 2, q, 0)

            for part, (q_done, k_done) in enumerate(((3, "part1"), (5, "part2"), (7, "parts_ready"))):
                sp.wait_ge(s("first_q"), q_done)
                stack_part(0, 0, 0, part, first_q_parts, (0,), s("fill_even0"))
                sp.wait_ge(s(k_done), 1)
                stack_part(0, 0, 1, part, parts[:, 1], (0,), s("fill_even0"))
            for half, par in ((0, 1), (1, 0), (1, 1)):
                for k in (1, 0):
                    for part in range(3):
                        stack_part(0, half, k, part, parts[:, 1] if k else first_q_parts, (par,),
                                   s(f"fill{half}") if par else s(f"fill_even{half}"))
            fill(1, 1, 0)
            pipeline(sp, iteration)

            for b in range(B):
                sp.wait_ge(s("x_new"), B + b + 1)
                sp.dma_start(out_dram[:, b], xs[:, b]).then_inc(s("st_out"), 16)
            sp.wait_ge(s("st_out"), 16 * B)

        @block.gpsimd
        def _(pool):
            nc.gpsimd.memset(minus_half[:], -0.5).then_inc(s("half_ready"), 1)

            def multiply(it, g):
                pool.wait_ge(s("cs_ready", g), it + 1)
                b, k = 4 * g + 3, slice(3 * T, 4 * T)
                for a in range(2):
                    last = nc.gpsimd.tensor_tensor(
                        tmp[:, g, 3, :, 64 * a:64 * a + 64].rearrange("p t (u d) -> p t u d", u=2),
                        st[:, b, :, 64 - 64 * a:128 - 64 * a].rearrange("p t (u d) -> p t u d", u=2),
                        coupling(g, k, a), ALU.mult)
                last.then_inc(s("mul_pool", g), 1)

            def update(it, g):
                multiply(it, g)
                pool.wait_ge(s("mul_pool", g), it + 1)
                nc.gpsimd.tensor_tensor(st[:, 4 * g + 3], st[:, 4 * g + 3], tmp[:, g, 3], ALU.add)\
                    .then_inc(s("upd_pool", g), 1)

            def invert(call, slots):
                pool.wait_ge(s("ln_var"), call + 1)
                nc.gpsimd.tensor_tensor(rstd[:, slots], var[:, slots], minus_half[:, slots], ALU.pow)\
                    .then_inc(s("ln_rstd"), 1)

            def cycles(n):
                with pool.Fori(0, CYCLES - 1) as c:
                    for g in range(G):
                        update(CYCLES * n + c, g)

            def rope_and_split(b, k):
                n = 2 * b + k - 1
                dst = parts_of(b, k)
                pool.wait_ge(s("q_done" if k == 0 else "k_done"), b + 1)
                nc.gpsimd.tensor_tensor(ra[:], qkf[:, k], cosb[:], ALU.mult).then_inc(s("rope_a"), 1)
                pool.wait_ge(s("swapped"), 1 if isinstance(b, int) and b == 0 else n + 2)
                nc.gpsimd.tensor_tensor(rb[:], qksw[:, k], sinb[:], ALU.mult).then_inc(s("rope_b"), 1)
                pool.wait_ge(s("rope_a"), n + 1)
                pool.wait_ge(s("rope_b"), n + 1)
                if not (isinstance(b, int) and b < 2):
                    for half in range(2):
                        pool.wait_ge(s(f"fill{half}"), filled(b))
                nc.gpsimd.tensor_tensor(dst[:, 0], ra[:], rb[:], ALU.add).then_inc(s("part1"), 1)
                nc.gpsimd.tensor_tensor(rc[:], ra[:], rb[:], ALU.add).then_inc(s("rope_c"), 1)
                pool.wait_ge(s("rope_c"), n + 1)
                pool.wait_ge(s("part1"), n + 1)
                nc.gpsimd.tensor_tensor(dst[:, 1], rc[:], dst[:, 0], ALU.subtract).then_inc(s("part2"), 1)
                nc.gpsimd.tensor_tensor(rd[:], rc[:], dst[:, 0], ALU.subtract).then_inc(s("res1"), 1)
                pool.wait_ge(s("res1"), n + 1)
                pool.wait_ge(s("part2"), n + 1)
                nc.gpsimd.tensor_tensor(dst[:, 2], rd[:], dst[:, 1], ALU.subtract)\
                    .then_inc(s("parts_ready"), 1)

            def iteration(i, q, first, last):
                if first >= 0 and last <= B - 3:
                    invert(B + i + 2, slice(q, q + 1))
                    rope_and_split(i + 2, 0)
                    rope_and_split(i + 2, 1)

            nc.gpsimd.memset(vst[:].rearrange("p q t h c -> p (q t h c)"), 0.0).then_inc(s("vst_zero"), 1)
            pool.wait_ge(s("half_ready"), 1)
            kst_words = kst[:].rearrange("p q h e c -> p q (h e c)").bitcast(F32)
            for b in range(B):
                invert(b, slice(b, b + 1))
                if b == 3:
                    nc.gpsimd.memset(kst_words[:, 0], 0.0)
            pool.wait_ge(s("vst_zero"), 1)
            nc.gpsimd.memset(vst[:].rearrange("p q t h c -> p (q t h) c")[:, :, DH:DH + 1], 1.0)\
                .then_inc(s("vst_one"), 1)
            nc.gpsimd.memset(orow[:], 1.0)
            nc.gpsimd.memset(kst_words[:, 1], 0.0).then_inc(s("setup_pool"), 1)
            cycles(0)
            multiply(CYCLES - 1, 0)
            for b in range(2):
                invert(B + b, slice(b, b + 1))
            pool.wait_ge(s("cst_in"), 32)
            pool.wait_ge(s("mul_done", 0), 3 * CYCLES)
            rope_and_split(0, 1)
            multiply(CYCLES - 1, 1)
            rope_and_split(1, 0)
            rope_and_split(1, 1)
            pipeline(pool, iteration)
            for pair in range(LAST_CALLS):
                invert(2 * B + pair, slice(2 * pair, 2 * pair + 2))
            cycles(1)
            for g in range(G):
                multiply(2 * CYCLES - 1, g)

        @block.vector
        def _(dve):
            nc.vector.memset(w3s[:], 0.0)
            nc.vector.memset(w4s[:], 0.0).then_inc(s("setup_dve"), 1)

            def token_stats(call, batches, slots):
                for src, k in zip(batches, range(slots.start, slots.stop)):
                    for t in range(T):
                        last = nc.vector.bn_stats(stats[:, k, t], src[:, t])
                if call is not None:
                    last.then_inc(s("ln_stats"), 1)

            def token_variance(call, slots):
                for k in range(slots.start, slots.stop):
                    for t in range(T):
                        last = nc.vector.bn_aggr(mv[:, k, t], stats[:, k, t])
                last.then_inc(s("ln_mv"), 1)
                dve.wait_ge(s("ln_mv"), call + 1)
                nc.vector.tensor_scalar(var[:, slots], mv[:, slots, :, 1], EPS, None, ALU.add)\
                    .then_inc(s("ln_var"), 1)

            def normalise_tokens(src, dst, slot, ready):
                for t in range(T):
                    last = nc.vector.tensor_scalar(dst[:, t], src[:, t], mv[:, slot, t, 0:1], rstd[:, slot, t:t + 1],
                                                   ALU.subtract, ALU.mult)
                last.then_inc(ready, 1)

            def first_variance(b):
                dve.wait_ge(s("x_first" if b == 0 else f"x_in{b // 2}"), 16)
                token_stats(b, [xs[:, b]], slice(b, b + 1))
                dve.wait_ge(s("ln_stats"), b + 1)
                token_variance(b, slice(b, b + 1))

            def normalise_state(call, b):
                dve.wait_ge(s("ln_rstd"), call + 1)
                normalise_tokens(xs[:, b], st[:, b], b, s("ln_out"))

            def pair_variance(pair):
                for b in (2 * pair, 2 * pair + 1):
                    token_stats(2 * B + pair if b % 2 else None, [xs[:, b]], slice(b, b + 1))
                dve.wait_ge(s("ln_stats"), 2 * B + pair + 1)
                token_variance(2 * B + pair, slice(2 * pair, 2 * pair + 2))

            def pair_normalise(pair):
                for b in (2 * pair, 2 * pair + 1):
                    normalise_state(2 * B + pair, b)

            def halves():
                dve.wait_ge(s("wc_in"), 16 * WC_DMAS)
                nc.vector.tensor_scalar(ar_tf[:], ar[:], TF_SHARE, None, ALU.mult)
                nc.vector.tensor_scalar(ar_gf[:], ar[:], GF_SHARE, None, ALU.mult)
                nc.vector.tensor_scalar(b4h[:], b4s[:], 0.5, None, ALU.mult)
                nc.vector.tensor_scalar(gb3h[:], gb3s[:], 0.5, None, ALU.mult)
                nc.vector.tensor_copy(g3r[:], g3s[:].to_broadcast([32, P])).then_inc(s("halves"), 1)

            def couple(it, g):
                dve.wait_ge(s("th_done", g), it + 1)
                waits_for(dve, s("mul_pool", g), it)
                nc.vector.scalar_tensor_tensor(
                    cs[:, g, 0].rearrange("p (b t) -> p b t", b=4), th[:, g], ar_tf[:],
                    s0[:, 4 * g:4 * g + 4].unsqueeze(2).to_broadcast([P, 4, T]), ALU.mult, ALU.add)\
                    .then_inc(s("cs0", g), 1)
                dve.wait_ge(s("cs0", g), it + 1)
                nc.vector.tensor_copy(cs[:, g, 2], cs[:, g, 0])
                nc.vector.tensor_scalar(cs[:, g, 1], cs[:, g, 0], -1.0, None, ALU.mult).then_inc(s("cs_ready", g), 1)
                dve.wait_ge(s("cs_ready", g), it + 1)

            def multiply(g, k):
                for a in range(2):
                    last = nc.vector.tensor_tensor(
                        tmp[:, g, k, :, 64 * a:64 * a + 64].rearrange("p t (u d) -> p t u d", u=2),
                        st[:, 4 * g + k, :, 64 - 64 * a:128 - 64 * a].rearrange("p t (u d) -> p t u d", u=2),
                        coupling(g, slice(T * k, T * k + T), a), ALU.mult)
                last.then_inc(s("mul_done", g), 1)

            def update(it, g):
                couple(it, g)
                for k in range(3):
                    multiply(g, k)
                for k in range(3):
                    dve.wait_ge(s("mul_done", g), 3 * it + k + 1)
                    nc.vector.tensor_tensor(st[:, 4 * g + k], st[:, 4 * g + k], tmp[:, g, k], ALU.add)\
                        .then_inc(s("upd_dve", g), 1)

            def add_half(v, b):
                x_b = xs[:, b].rearrange("p t d -> p (t d)")
                return nc.vector.scalar_tensor_tensor(x_b, v.rearrange("p t d -> p (t d)"), 0.5, x_b,
                                                      ALU.mult, ALU.add)

            def add_state(n, g):
                for k in range(4):
                    if k < 3:
                        dve.wait_ge(s("upd_dve", g), 3 * (CYCLES - 1) * (n + 1) - 2 + k)
                    else:
                        dve.wait_ge(s("upd_pool", g), (CYCLES - 1) * (n + 1))
                    add_half(st[:, 4 * g + k], 4 * g + k).then_inc(s("half_added", g), 1)

            def finish(n, g, k):
                if k < 3:
                    dve.wait_ge(s("mul_done", g), 3 * (CYCLES * (n + 1) - 1) + k + 1)
                else:
                    dve.wait_ge(s("mul_pool", g), CYCLES * (n + 1))
                dve.wait_ge(s("half_added", g), 4 * n + k + 1)
                add_half(tmp[:, g, k], 4 * g + k).then_inc(s("x_new"), 1)

            def cycles(n):
                for c in range(CYCLES - 1):
                    for g in range(G):
                        if c == 0:
                            dve.wait_ge(s("gth_done", g), n + 1)
                            nc.vector.tensor_scalar(s0[:, 4 * g:4 * g + 4], gth[:, 4 * g:4 * g + 4], ar_gf[:],
                                                    BASE_COUPLING, ALU.mult, ALU.add).then_inc(s("s0_ready", g), 1)
                            dve.wait_ge(s("s0_ready", g), n + 1)
                        update(CYCLES * n + c, g)
                        if c == CYCLES - 2:
                            add_state(n, g)

            def row_max(i, q, u, c):
                _, _, n, h = ahead(i, q, u)
                dve.wait_ge(s("s_ready"), 2 * n + c + 1)
                half, hl = h // HALF, h % HALF
                nc.vector.tensor_reduce(nmax[:, half, 2 * c:2 * c + 2, hl % 2, hl // 2:hl // 2 + 1],
                                        ps[:, 2 + 2 * c:4 + 2 * c, :], AX_X, ALU.max, negate=True)\
                    .then_inc(s("s_used"), 1)

            def split_max(b, half):
                n = 2 * b + half
                dve.wait_ge(s("s_used"), 2 * (b * H + (half + 1) * HALF))
                waits_for(dve, s("maxT_ready"), n)
                m = nmax[:, half]
                nc.vector.tensor_copy(nparts[:, :, :, 0], m).then_inc(s("n1"), 1)
                dve.wait_ge(s("n1"), n + 1)
                nc.vector.tensor_tensor(nres[:], m, nparts[:, :, :, 0], ALU.subtract).then_inc(s("nr1"), 1)
                dve.wait_ge(s("nr1"), n + 1)
                nc.vector.tensor_copy(nparts[:, :, :, 1], nres[:]).then_inc(s("n2"), 1)
                dve.wait_ge(s("n2"), n + 1)
                nc.vector.tensor_tensor(nparts[:, :, :, 2], nres[:], nparts[:, :, :, 1], ALU.subtract)\
                    .then_inc(s("n3"), 1)

            def normalise(i, lt):
                n = (i - 1) * T + lt
                dve.wait_ge(s("oT_ready"), n + 1)
                o = ps[:, 7, :].rearrange("p (h c) -> p h c", c=VC)
                nc.vector.reciprocal(rden[:, lt, :], o[:, :, DH]).then_inc(s("oT_rden"), 1)
                dve.wait_ge(s("oT_rden"), n + 1)
                waits_for(dve, s("onT_ready"), i - 1)
                nc.vector.tensor_tensor(on[:, lt].rearrange("p (h d) -> p h d", d=DH), o[:, :, 0:DH],
                                        rden[:, lt].unsqueeze(2).to_broadcast([P, H, DH]), ALU.mult)\
                    .then_inc(s("oT_used"), 1)

            def residual(i):
                dve.wait_ge(s("proj_ready"), i)
                nc.vector.tensor_tensor(batch_of(xs, i - 1), ps[:, 7, :], batch_of(xs, i - 1), ALU.add)\
                    .then_inc(s("proj_done"), 1)

            def batch_of(v, b):
                if isinstance(b, int):
                    return v[:, b].rearrange("p t d -> p (t d)")
                return v[:].rearrange("p b t d -> p (b t d)")[:, bass.ds(b * (T * D), T * D)]

            def swap(b, k):
                nc.vector.stream_shuffle(qksw[:, k], qkf[:, k], SWAPPED).then_inc(s("swapped"), 1)

            def iteration(i, q, first, last):
                a_on = first >= 0 and last <= B - 3
                b = i + 2
                tokens = batch_of(xs, b).rearrange("p (t d) -> p t d", t=T) if a_on else None
                for u in range(H):
                    s_on = maxima_on(first, last, u)
                    if a_on and u == 0:
                        token_stats(B + b, [tokens], slice(q, q + 1))
                    if a_on and u == 1:
                        dve.wait_ge(s("ln_stats"), B + b + 1)
                    if first >= 1 and u - 1 in OUTPUT_AT:
                        normalise(i, OUTPUT_AT[u - 1])
                    if s_on:
                        row_max(i, q, u, 0)
                    if a_on and u == 1:
                        token_variance(B + b, slice(q, q + 1))
                    if u == H - LEAD and first >= 0 and last <= B - 1:
                        split_max(i, 1)
                    if u == H - LEAD + HALF and first >= -1 and last <= B - 2:
                        split_max(i + 1, 0)
                    if first >= 1 and u == 15:
                        residual(i)
                    if a_on and u in (5, 6):
                        dve.wait_ge(s("qk"[u - 5] + "_done"), b + 1)
                    if s_on:
                        row_max(i, q, u, 1)
                    if a_on and u == 1:
                        dve.wait_ge(s("ln_rstd"), B + b + 1)
                        waits_for(dve, s("xT_ready"), b - 1)
                        normalise_tokens(tokens, xn[:, q], q, s("xn_ready"))
                    if a_on and u in (5, 6):
                        swap(b, u - 5)
                    if first >= B - 1 and last <= B - 1:
                        next_tokens(u)
                        if u % 4 == 3:
                            take_pv(i, q, u)
                    if first >= B and u == 3:
                        take_pv(i, q, u)
                    if first >= B and u == 13:
                        pair_normalise(LAST_CALLS - 2)

            def take_pv(i, q, u):
                nc.vector.tensor_copy(*wait_for_pv(dve, i, q, u)).then_inc(s("pv_used"), 1)

            def next_tokens(u):
                if u == H - LEAD:
                    dve.wait_ge(s("proj_done"), B - 2)
                if H - LEAD <= u < H - LEAD + LAST_CALLS - 1:
                    pair_variance(u - (H - LEAD))
                if u in (9, 13):
                    pair_normalise((u - 9) // 4)

            def first_norm(b):
                dve.wait_ge(s("x_new"), b + 1)
                token_stats(B + b, [xs[:, b]], slice(b, b + 1))
                dve.wait_ge(s("ln_stats"), B + b + 1)
                token_variance(B + b, slice(b, b + 1))

            def first_normalise(b):
                dve.wait_ge(s("ln_rstd"), B + b + 1)
                normalise_tokens(xs[:, b], xn[:, b], b, s("xn_ready"))

            def rope_and_split_first_q():
                fa, fb, fc, fd = (xT[:, 0, j] for j in range(4))
                dve.wait_ge(s("cst_in"), 32)
                dve.wait_ge(s("k_done"), 1)
                swap(0, 1)
                dve.wait_ge(s("q_done"), 1)
                swap(0, 0)
                nc.vector.tensor_tensor(fa, qkf[:, 0], cosb[:], ALU.mult).then_inc(s("first_q"), 1)
                dve.wait_ge(s("swapped"), 2)
                nc.vector.tensor_tensor(fb, qksw[:, 0], sinb[:], ALU.mult).then_inc(s("first_q"), 1)
                dve.wait_ge(s("first_q"), 2)
                nc.vector.tensor_tensor(first_q_parts[:, 0], fa, fb, ALU.add).then_inc(s("first_q"), 1)
                nc.vector.tensor_tensor(fc, fa, fb, ALU.add).then_inc(s("first_q"), 1)
                dve.wait_ge(s("first_q"), 4)
                nc.vector.tensor_tensor(first_q_parts[:, 1], fc, first_q_parts[:, 0], ALU.subtract)\
                    .then_inc(s("first_q"), 1)
                nc.vector.tensor_tensor(fd, fc, first_q_parts[:, 0], ALU.subtract).then_inc(s("first_q"), 1)
                dve.wait_ge(s("first_q"), 6)
                nc.vector.tensor_tensor(first_q_parts[:, 2], fd, first_q_parts[:, 1], ALU.subtract).then_inc(s("first_q"), 1)

            for b in range(B + 1):
                if b < B:
                    first_variance(b)
                if b == B - 2:
                    halves()
                if b > 0:
                    normalise_state(b - 1, b - 1)
            nc.vector.tensor_copy(ident_bf[:], ident[:]).then_inc(s("ident_ready"), 1)
            dve.wait_ge(s("halves"), 1)
            cycles(0)
            couple(CYCLES - 1, 0)
            multiply(0, 0)
            finish(0, 0, 0)
            first_norm(0)
            multiply(0, 1)
            first_normalise(0)
            multiply(0, 2)
            for k in range(1, 4):
                finish(0, 0, k)
            first_norm(1)
            rope_and_split_first_q()
            first_normalise(1)
            couple(CYCLES - 1, 1)
            for k in range(3):
                multiply(1, k)
            for k in range(4):
                finish(0, 1, k)
            for k in range(2):
                dve.wait_ge(s("qk"[k] + "_done"), 2)
                swap(1, k)
            dve.wait_ge(s("x_new"), B)
            pipeline(dve, iteration)
            iteration(B - 1, 1, B - 1, B - 1)
            dve.wait_ge(s("proj_done"), B - 1)
            token_stats(None, [xs[:, B - 2]], slice(B - 2, B - 1))
            iteration(B, 0, B, B)
            dve.wait_ge(s("proj_done"), B)
            last_call = 2 * B + LAST_CALLS - 1
            token_stats(last_call, [xs[:, B - 1]], slice(B - 1, B))
            dve.wait_ge(s("ln_stats"), last_call + 1)
            token_variance(last_call, slice(B - 2, B))
            pair_normalise(LAST_CALLS - 1)
            cycles(1)
            for g in range(G):
                couple(2 * CYCLES - 1, g)
                for k in range(3):
                    multiply(g, k)
                for k in range(4):
                    finish(1, g, k)

        @block.scalar
        def _(act):
            def evacuate(dst, src):
                return nc.scalar.activation(dst, src, ACT.Copy)

            def turned(it, g, ks=range(4), first=False):
                for k in ks:
                    act.wait_ge(s("T_ready", g), 4 * it + k + 1)
                    nc.scalar.activation(xT[:, g, k], ps[:, 4 * g + k, :], ACT.Copy,
                                         accum_out=gm[:, 4 * g + k:4 * g + k + 1] if first else None)\
                        .then_inc(s("T_copied", g), 1)

            def gelu1(it, g, ks):
                for k in ks:
                    act.wait_ge(s("L1_ready", g), 4 * it + k + 1)
                    nc.scalar.activation(h1[:, g, k], ps[:, 4 * g + k, :], ACT.Gelu, bias=b1s[:])\
                        .then_inc(s("h1_done", g), 1)

            def gelu2(it, g, ks=(0, 1)):
                for k in ks:
                    act.wait_ge(s("L2_ready", g), 2 * it + k + 1)
                    nc.scalar.activation(h2[:, g, k], ps[:, 4 * g + k, :], ACT.Gelu, bias=b2s[:])\
                        .then_inc(s("h2_done", g), 1)

            def gelu3(it, g):
                act.wait_ge(s("L3_ready", g), it + 1)
                nc.scalar.activation(h3[:, g], ps[:, 4 * g + 2, :], ACT.Gelu, bias=b3s[:]).then_inc(s("h3_done", g), 1)

            def tanh(it, g):
                act.wait_ge(s("L4_ready", g), it + 1)
                nc.scalar.activation(th[:, g].rearrange("p b t -> p t b"),
                                     ps[:, 4 * g + 3, 0:4 * T].rearrange("p (t b) -> p t b", b=4),
                                     ACT.Tanh, bias=b4h[:], scale=0.5).then_inc(s("th_done", g), 1)

            def global1(n, g):
                act.wait_ge(s("gh1_ready", g), n + 1)
                nc.scalar.activation(gh1[:, 4 * g:4 * g + 4], global_out(g, 0)[0:64], ACT.Gelu, bias=gb1s[:],
                                     scale=1.0 / S).then_inc(s("gh1_done", g), 1)

            def global2(n, g):
                act.wait_ge(s("gh2_ready", g), n + 1)
                nc.scalar.activation(gh2[:, 4 * g:4 * g + 4], global_out(g, 1)[0:32], ACT.Gelu, bias=gb2s[:])\
                    .then_inc(s("gh2_done", g), 1)

            def global3(n, g):
                act.wait_ge(s("gth_ready", g), n + 1)
                nc.scalar.activation(gth[:, 4 * g:4 * g + 4], global_out(g, 2), ACT.Tanh, bias=gb3h[:], scale=0.5)\
                    .then_inc(s("gth_done", g), 1)

            def first_cycle(n):
                it = CYCLES * n
                turned(it, 0, (0, 1), True)
                if n == 0:
                    act.wait_ge(s("w1_in"), 32)
                    gelu1(it, 0, (0, 1))
                turned(it, 0, (2, 3), True)
                gelu1(it, 0, (2, 3) if n == 0 else range(4))
                if n == 0:
                    act.wait_ge(s("w2_in"), 32)
                gelu2(it, 0, (0,))
                if n == 1:
                    take_onT(B)
                gelu2(it, 0, (1,))
                if n == 0:
                    act.wait_ge(s("wc_in"), 16 * WC_DMAS)
                global1(n, 0)
                turned(it, 1, (0, 1), True)
                gelu3(it, 0)
                global2(n, 0)
                gelu1(it, 1, (0,))
                act.wait_ge(s("halves"), 1)
                tanh(it, 0)
                global3(n, 0)
                gelu1(it, 1, (1,))
                turned(it, 1, (2, 3), True)
                gelu1(it, 1, (2, 3))
                global1(n, 1)
                gelu2(it, 1, (0,))
                global2(n, 1)
                gelu2(it, 1, (1,))
                global3(n, 1)

            def feed_forward(n):
                first_cycle(n)
                with act.Fori(1, CYCLES) as c:
                    it = CYCLES * n + c
                    for g in range(G):
                        turned(it, g)
                        gelu3(it - (g == 0), 1 - g)
                        tanh(it - (g == 0), 1 - g)
                        gelu1(it, g, range(4))
                        gelu2(it, g)

            def exps(i, u, tiles):
                for mt in tiles:
                    act.wait_ge(s("st_ready"), (i * H + u) * T + mt + 1)
                    if mt == 0 and u % 4 == 0:
                        waits_for(act, s("pv_ready"), 4 * i + u // 4 - 1)
                    nc.scalar.activation(probs[:, u % 8, S * mt:S * (mt + 1)], ps[:, score_bank(i, u, mt), :],
                                         ACT.Exp, scale=SCALE).then_inc(s("exp_done"), 1)

            def take_pv(i, q, u):
                evacuate(*wait_for_pv(act, i, q, u)).then_inc(s("pv_used"), 1)

            def take_side_work(i, q, u, first, last):
                if first >= 0 and last <= B - 3:
                    b = i + 2
                    if u == 2:
                        act.wait_ge(s("xT_ready"), b + 1)
                        evacuate(xnT[:, q], ps[:, 7, :]).then_inc(s("xnT_done"), 1)
                    if u in (3, 4):
                        k = u - 3
                        act.wait_ge(s("qk"[k] + "_ready"), b + 1)
                        waits_for(act, s("rope_b"), 2 * b - 2 + k)
                        evacuate(qkf[:, k], ps[:, 7, :]).then_inc(s("qk"[k] + "_done"), 1)
                if u == 5 and first >= 0 and last <= B - 1:
                    take_max(i, 1)
                if u == 13 and first >= -1 and last <= B - 2:
                    take_max(i + 1, 0)
                if u == 7 and first >= -1 and last <= B - 2:
                    act.wait_ge(s("v_ready"), i + 2)
                    evacuate(vst[:, 1 - q, :, :, 0:DH].rearrange("p t h d -> p (t h) d"),
                             ps[:, 7, :].rearrange("p (a d) -> p a d", d=DH)).then_inc(s("v_done"), 1)
                if u == 12 and first >= 1:
                    take_onT(i)

            def iteration(i, q, first, last):
                for u in range(H):
                    if first >= 0 and last <= B - 1:
                        exps(i, u, (0, 1))
                    if u > 0:
                        take_side_work(i, q, u - 1, first, last)
                    if first >= 0 and last <= B - 1:
                        exps(i, u, (2, 3))
                    if u == 6 and first >= 0 and last <= B - 1:
                        max_rows(i, q, 1)
                    if u == 14 and first >= -1 and last <= B - 2:
                        max_rows(i + 1, 1 - q, 0)
                    if u % 4 == 3:
                        if (u > 3 and first >= 0 and last <= B - 2) or (u == 3 and first >= 1 and last <= B - 2):
                            take_pv(i, q, u)

            def take_onT(i):
                act.wait_ge(s("onT_ready"), i)
                waits_for(act, s("proj_ready"), i - 1)
                evacuate(onT, ps[:, 7, :]).then_inc(s("onT_done"), 1)

            def take_max(b, half):
                n = 2 * b + half
                act.wait_ge(s("maxT_ready"), n + 1)
                waits_for(act, s(f"mrow_out{1 - half}"), 16 * (b + half))
                evacuate(mrow[:], ps[0:6 * PAIRS, 7, 0:S // 2].bitcast(BF16)).then_inc(s("maxT_done"), 1)

            def max_rows(b, q, half):
                act.wait_ge(s("maxT_done"), 2 * b + half + 1)
                act.dma_start(qst[MAX_ROW:ROWS, q, PAIRS * half:PAIRS * (half + 1), :], mrow[:])\
                    .then_inc(s(f"mrow_out{half}"), 16)

            feed_forward(0)
            act.wait_ge(s("wT_ready"), 1)
            evacuate(wT[:].rearrange("p a c -> p (a c)"), ps[:, 1, :]).then_inc(s("wT_copied"), 1)
            gelu3(CYCLES - 1, 1)
            for b in range(2):
                act.wait_ge(s("xT_ready"), b + 1)
                evacuate(xnT[:, b], ps[:, 0, :]).then_inc(s("xnT_done"), 1)
                if b == 0:
                    tanh(CYCLES - 1, 1)
                for k in (1, 0) if b == 0 else (0, 1):
                    act.wait_ge(s("qk"[k] + "_ready"), b + 1)
                    if b == 1 and k == 0:
                        act.wait_ge(s("first_q"), 2)
                    if b == 1 and k == 1:
                        act.wait_ge(s("rope_b"), 1)
                    evacuate(qkf[:, k], ps[:, 1 - k, :]).then_inc(s("qk"[k] + "_done"), 1)
            pipeline(act, iteration)
            iteration(B - 1, 1, B - 1, B - 1)
            feed_forward(1)
            gelu3(2 * CYCLES - 1, 1)
            tanh(2 * CYCLES - 1, 1)

        @block.tensor
        def _(pe):
            def turn(it, n, g, k, first):
                if first:
                    pe.wait_ge(s("ln_out"), B * n + 4 * g + k + 1)
                elif k < 3:
                    pe.wait_ge(s("upd_dve", g), 3 * (it - n) - 2 + k)
                else:
                    pe.wait_ge(s("upd_pool", g), it - n)
                for t in range(T):
                    last = nc.tensor.transpose(ps[:, 4 * g + k, P * t:P * t + P], st[:, 4 * g + k, t], ident[:])
                last.then_inc(s("T_ready", g), 1)

            def layer1(it, g, ks):
                for k in ks:
                    pe.wait_ge(s("T_copied", g), 4 * it + k + 1)
                    nc.tensor.matmul(ps[:, 4 * g + k, :], w1s[:], xT[:, g, k], start=True, stop=True)\
                        .then_inc(s("L1_ready", g), 1)

            def layer2(it, g, pairs=(0, 1)):
                for pr in pairs:
                    pe.wait_ge(s("h1_done", g), 4 * it + 2 * pr + 2)
                    for k in range(2):
                        last = nc.tensor.matmul(ps[64 * k:64 * k + 64, 4 * g + pr, :], w2s[:], h1[:, g, 2 * pr + k],
                                                start=True, stop=True)
                    last.then_inc(s("L2_ready", g), 1)

            def layer3(it, g):
                pe.wait_ge(s("h2_done", g), 2 * it + 2)
                for pr in range(2):
                    last = nc.tensor.matmul(ps[64 * pr:64 * pr + 64, 4 * g + 2, :], w3s[:], h2[:, g, pr],
                                            start=True, stop=True)
                last.then_inc(s("L3_ready", g), 1)

            def layer4(it, g):
                pe.wait_ge(s("h3_done", g), it + 1)
                for t in range(T):
                    last = nc.tensor.matmul(ps[:, 4 * g + 3, 4 * t:4 * t + 4], h3[:, g, P * t:P * t + P], w4s[:],
                                            start=True, stop=True)
                last.then_inc(s("L4_ready", g), 1)

            def global1(n, g):
                pe.wait_ge(s("T_copied", g), 4 * CYCLES * n + 4)
                if g == 0:
                    pe.wait_ge(s("h2_done", 0), 2 * CYCLES * n + 1)
                nc.tensor.matmul(global_out(g, 0)[0:64], g1s[:], gm[:, 4 * g:4 * g + 4], start=True, stop=True)\
                    .then_inc(s("gh1_ready", g), 1)

            def global2(n, g):
                pe.wait_ge(s("gh1_done", g), n + 1)
                if g == 1:
                    pe.wait_ge(s("gth_done", 0), n + 1)
                nc.tensor.matmul(global_out(g, 1)[0:32], g2s[:], gh1[:, 4 * g:4 * g + 4], start=True, stop=True)\
                    .then_inc(s("gh2_ready", g), 1)

            def global3(n, g):
                pe.wait_ge(s("gh2_done", g), n + 1)
                nc.tensor.matmul(global_out(g, 2), g3r[:], gh2[:, 4 * g:4 * g + 4], start=True, stop=True)\
                    .then_inc(s("gth_ready", g), 1)

            def first_cycle(n):
                it = CYCLES * n

                def between(u):
                    if n == 1:
                        side_work(B, 0, u, B, B)

                def turns(g, ks):
                    for k in ks:
                        turn(it, n, g, k, True)

                if n == 0:
                    turns(0, (0, 1))
                    pe.wait_ge(s("w1_in"), 32)
                else:
                    for k in range(4):
                        pe.wait_ge(s("exp_done"), B * H * T - 3 + k)
                        turns(0, (k,))
                    for u in range(T):
                        products(B, 0, u)
                for k in range(4):
                    layer1(it, 0, (k,))
                    between(list(OUTPUT_AT)[k])
                    if n == 0 and k == 1:
                        turns(0, (2, 3))
                if n == 0:
                    pe.wait_ge(s("w2_in"), 32)
                layer2(it, 0, (0,))
                between(12)
                layer2(it, 0, (1,))
                between(14)
                if n == 0:
                    turns(1, (0, 1))
                    pe.wait_ge(s("wc_in"), 16 * WC_DMAS)
                global1(n, 0)
                if n == 1:
                    turns(1, (0, 1))
                layer3(it, 0)
                global2(n, 0)
                layer1(it, 1, (0,))
                layer4(it, 0)
                pe.wait_ge(s("halves"), 1)
                global3(n, 0)
                layer1(it, 1, (1,))
                turns(1, (2, 3))
                layer1(it, 1, (2, 3))
                global1(n, 1)
                layer2(it, 1, (0,))
                global2(n, 1)
                layer2(it, 1, (1,))
                global3(n, 1)

            def feed_forward(n):
                first_cycle(n)
                with pe.Fori(1, CYCLES) as c:
                    it = CYCLES * n + c
                    for g in range(G):
                        for k in range(4):
                            if g == 0 and k == 1:
                                pe.wait_ge(s("gth_done", 1), n + 1)
                            turn(it, n, g, k, False)
                        layer3(it - (g == 0), 1 - g)
                        layer1(it, g, (0,))
                        layer4(it - (g == 0), 1 - g)
                        layer1(it, g, (1, 2, 3))
                        layer2(it, g)

            def scores_T(i, q, u, mt):
                n = (i * H + u) * T + mt
                if u % HALF == 0 and mt == 0:
                    pe.wait_ge(s(f"mrow_out{u // HALF}"), 16 * i + 16)
                if last_heads(i, u) and not last_heads(i, u - 1) and mt >= 2:
                    pe.wait_ge(s("s_used"), 2 * B * H)
                elif last_heads(i, u - 1) and u > 0:
                    pe.wait_ge(s("exp_done"), n - 3)
                else:
                    waits_for(pe, s("exp_done"), n - 1)
                nc.tensor.matmul(ps[:, score_bank(i, u, mt), :], kst[:, q, u // 2, u % 2, P * mt:P * mt + P],
                                 qst[:, q, u // 2, :], start=True, stop=True).then_inc(s("st_ready"), 1)

            def scores(i, q, u, lt):
                b, qb, n, h = ahead(i, q, u)
                if lt == 0 and even_first(b):
                    if h % HALF == 0:
                        pe.wait_ge(s(f"fill_even{h // HALF}"), FILL // 2)
                    if h % HALF == 1:
                        pe.wait_ge(s(f"fill{h // HALF}"), filled(1))
                elif lt == 0 and h % HALF == 0:
                    pe.wait_ge(s(f"fill{h // HALF}"), filled(b + 1))
                if lt % 2 == 0:
                    waits_for(pe, s("s_used"), 2 * n + lt // 2 - 1)
                rows = slice(0, HEAD_ROWS if even_first(b) and h % 2 == 0 else MAX_ROW)
                mm = nc.tensor.matmul(ps[:, 2 + lt, :], qst[rows, qb, h // 2, P * lt:P * lt + P],
                                      kst[rows, qb, h // 2, h % 2, :], start=True, stop=True)
                if lt % 2 == 1:
                    mm.then_inc(s("s_ready"), 1)

            def products(i, q, u):
                g = u // 4 - 1
                b, qb = (i, q) if g >= 0 else (i - 1, 1 - q)
                g, mt = g % 4, u % 4
                if mt == 0:
                    pe.wait_ge(s("exp_done"), (4 * b + g + 1) * 4 * T)
                    waits_for(pe, s("pv_used"), 4 * b + g)
                    if g == 0:
                        pe.wait_ge(s("v_done"), b + 1)
                for j in range(4):
                    h = 4 * g + j
                    last = nc.tensor.matmul(ps[32 * j:32 * j + 32, 6, :], vst[:, qb, mt, h, :],
                                            probs[:, h % 8, S * mt:S * mt + S], start=(mt == 0), stop=(mt == T - 1))
                if mt == T - 1:
                    last.then_inc(s("pv_ready"), 1)

            def project(b, w, ready, xq):
                nc.tensor.matmul(ps[:, 7, :], wT[:, w], xnT[:, xq], start=True, stop=True).then_inc(s(ready), 1)

            def turn_max(b, half):
                pe.wait_ge(s("n3"), 2 * b + half + 1)
                for t in range(T):
                    last = nc.tensor.transpose(ps[0:6 * PAIRS, 7, 0:S // 2].bitcast(BF16)[:, P * t:P * t + P],
                                               nparts[:, t].rearrange("p a k h -> p (a k h)"), ident_bf[:])
                last.then_inc(s("maxT_ready"), 1)

            def side_work(i, q, u, first, last_i):
                a_on = first >= 0 and last_i <= B - 3
                c_on = first >= 1
                if u == 2 and a_on:
                    b = i + 2
                    waits_for(pe, s("proj_done"), i - 1)
                    waits_for(pe, s("maxT_done"), 2 * (i + 1) - 1)
                    waits_for(pe, s("v_done"), i + 1)
                    waits_for(pe, s("k_done"), i + 2)
                    pe.wait_ge(s("xn_ready"), b + 1)
                    for t in range(T):
                        last = nc.tensor.transpose(ps[:, 7, P * t:P * t + P], xn[:, q, t], ident[:])
                    last.then_inc(s("xT_ready"), 1)
                if u == 3 and a_on:
                    pe.wait_ge(s("xnT_done"), i + 3)
                    project(i + 2, 0, "q_ready", q)
                if u == 4 and a_on:
                    pe.wait_ge(s("q_done"), i + 3)
                    project(i + 2, 1, "k_ready", q)
                if u == 5 and first >= 0 and last_i <= B - 1:
                    waits_for(pe, s("k_done"), i + 3 if a_on else 0)
                    waits_for(pe, s("proj_done"), i - 1 if not a_on else 0)
                    turn_max(i, 1)
                if u == 7 and first >= -1 and last_i <= B - 2:
                    waits_for(pe, s("oT_used"), T * (i - 1) + 1 if c_on else 0)
                    waits_for(pe, s("k_done"), i + 3 if a_on else 0)
                    waits_for(pe, s("maxT_done"), 2 * i + 2 if first >= 0 else 0)
                    for t in range(T):
                        last = nc.tensor.matmul(ps[:, 7, P * t:P * t + P], xnT[:, 1 - q, P * t:P * t + P], wT[:, 2],
                                                start=True, stop=True)
                    last.then_inc(s("v_ready"), 1)
                if c_on and u in OUTPUT_AT:
                    lt = OUTPUT_AT[u]
                    if lt == 0:
                        pe.wait_ge(s("pv_used"), 4 * i)
                        waits_for(pe, s("proj_done"), i - 1)
                        waits_for(pe, s("maxT_done"), 2 * i + 2 if last_i <= B - 1 else 0)
                    waits_for(pe, s("v_done"), i + 2 if lt == 1 and last_i <= B - 2 else 0)
                    waits_for(pe, s("oT_used"), T * (i - 1) + lt)
                    for g in range(4):
                        last = nc.tensor.transpose(ps[:, 7, P * g:P * g + P], output_T(g, 1 - q)[:, P * lt:P * lt + P], ident[:])
                    last.then_inc(s("oT_ready"), 1)
                if c_on and u == 12:
                    pe.wait_ge(s("oT_used"), T * i)
                    for t in range(T):
                        last = nc.tensor.transpose(ps[:, 7, P * t:P * t + P], on[:, t], ident[:])
                    last.then_inc(s("onT_ready"), 1)
                if c_on and u == 14:
                    pe.wait_ge(s("onT_done"), i)
                    waits_for(pe, s("maxT_done"), 2 * i + 3 if last_i <= B - 2 else 0)
                    for t in range(T):
                        last = nc.tensor.matmul(ps[:, 7, P * t:P * t + P], onT[:, P * t:P * t + P], wT[:, 3],
                                                start=True, stop=True)
                    last.then_inc(s("proj_ready"), 1)
                if u == 13 and first >= -1 and last_i <= B - 2:
                    waits_for(pe, s("onT_done"), i if c_on else 0)
                    pe.wait_ge(s("v_done"), i + 2)
                    turn_max(i + 1, 0)

            def iteration(i, q, first, last):
                for u in range(H):
                    st_on = first >= 0 and last <= B - 1
                    s_on = maxima_on(first, last, u)
                    pv_on = (u >= 4 and st_on) or (u < 4 and first >= 1)
                    for t in (0, 1):
                        if st_on:
                            scores_T(i, q, u, t)
                        if s_on:
                            scores(i, q, u, t)
                    if pv_on:
                        products(i, q, u)
                    for t in (2, 3):
                        if st_on:
                            scores_T(i, q, u, t)
                        if s_on:
                            scores(i, q, u, t)
                    side_work(i, q, u, first, last)

            pe.wait_ge(s("ident_in"), 16)
            feed_forward(0)
            pe.wait_ge(s("w_in"), 16 * 10)
            for j in range(4):
                last = nc.tensor.transpose(ps[:, 1, P * j:P * j + P], wnat[:, j], ident[:])
            last.then_inc(s("wT_ready"), 1)
            layer3(CYCLES - 1, 1)
            for b in range(2):
                pe.wait_ge(s("xn_ready"), b + 1)
                waits_for(pe, s("k_done"), b)
                for t in range(T):
                    last = nc.tensor.transpose(ps[:, 0, P * t:P * t + P], xn[:, b, t], ident[:])
                last.then_inc(s("xT_ready"), 1)
                if b == 0:
                    layer4(CYCLES - 1, 1)
                    pe.wait_ge(s("wT_copied"), 1)
                pe.wait_ge(s("xnT_done"), b + 1)
                waits_for(pe, s("q_done"), b)
                for k in (1, 0) if b == 0 else (0, 1):
                    nc.tensor.matmul(ps[:, 1 - k, :], wT[:, k], xnT[:, b], start=True, stop=True)\
                        .then_inc(s("qk"[k] + "_ready"), 1)
            pe.wait_ge(s("th_done", 1), CYCLES)
            pe.wait_ge(s("ident_ready"), 1)
            pe.wait_ge(s("vst_one"), 1)
            pe.wait_ge(s("ones_dma"), 16 * 4)
            pipeline(pe, iteration)
            iteration(B - 1, 1, B - 1, B - 1)
            feed_forward(1)
            layer3(2 * CYCLES - 1, 1)
            layer4(2 * CYCLES - 1, 1)


_INS = ['L0_attn_x', 'L0_attn_w_qkv', 'L0_attn_w_out',
        'L0_ffn_cn_w1', 'L0_ffn_cn_b1', 'L0_ffn_cn_w2', 'L0_ffn_cn_b2',
        'L0_ffn_cn_w3', 'L0_ffn_cn_b3', 'L0_ffn_cn_w4', 'L0_ffn_cn_b4',
        'L0_ffn_gc_w1', 'L0_ffn_gc_b1', 'L0_ffn_gc_w2', 'L0_ffn_gc_b2', 'L0_ffn_gc_w3', 'L0_ffn_gc_b3',
        'L0_ffn_adaptive_range']


def shape_constants(S, D, H):
    import numpy as np
    dh = D // H
    half = dh // 2
    inv_freq = (np.float32(1.0) / np.float32(10000.0) ** (np.arange(half, dtype=np.float32) / np.float32(half)))
    ang = np.arange(S, dtype=np.float32)[:, None] * inv_freq.astype(np.float32)[None, :]
    cos, sin = np.cos(ang).astype(np.float32).T, np.sin(ang).astype(np.float32).T
    cos = np.tile(np.repeat(np.concatenate([cos, cos]), H // 4, axis=0), (4, 1))
    sin = np.tile(np.repeat(np.concatenate([-sin, sin]), H // 4, axis=0), (4, 1))
    return (np.ascontiguousarray(cos), np.ascontiguousarray(sin), np.eye(128, dtype=np.float32))


def kernel(**inputs):
    import numpy as _np
    import concourse.bacc as _bacc
    from concourse import mybir as _mybir
    from concourse.bass_utils import run_bass_kernel_spmd as _run

    nc = _bacc.Bacc("TRN2", target_bir_lowering=False, num_devices=1)
    arrays, args = {}, []

    def give(name, a):
        arrays[name] = a
        return nc.dram_tensor(name, a.shape, _mybir.dt.from_np(a.dtype), kind="ExternalInput").ap()

    for name in _INS:
        args.append(give(f"in_{name}_dram", _np.ascontiguousarray(inputs[name])))
    B, S, D = inputs['L0_attn_x'].shape
    tables = [give(f"in_{n}_dram", a) for n, a in zip(("cos", "sin", "ident"), shape_constants(S, D, 16))]
    out = nc.dram_tensor("out_0_dram", (B, S, D), _mybir.dt.float32, kind="ExternalOutput").ap()
    macaron_kernel(nc, args[0], args[1], args[2], args[3:11], args[11:17], args[17], *tables, out)
    r = _run(nc, [arrays], core_ids=[0])
    return r.results[0]["out_0_dram"]
```
